# Optimizing a Trainium2 kernel written in Bass

```python
import numpy as np
import jax
import jax.numpy as jnp

def _softmax(x, axis=-1):
    return jax.nn.softmax(x, axis=axis)

def _gelu(x):
    return jax.nn.gelu(x, approximate=True)

def _silu(x):
    return jax.nn.silu(x)

def _sigmoid(x):
    return jax.nn.sigmoid(x)

def _layernorm(x, axis=-1, eps=1e-05):
    m = jnp.mean(x, axis=axis, keepdims=True)
    v = jnp.var(x, axis=axis, keepdims=True)
    return (x - m) / jnp.sqrt(v + eps)

def _scatter_add(tgt, idx, src, axis=0):
    return tgt.at[idx].add(src)

def _segment_sum(src, seg, n):
    return jax.ops.segment_sum(src, seg, n)
kernel_name = 'mk_gnn_ffn_d1_gnn_r32_e99859'

def setup_inputs(seed: int=0):
    np.random.seed(seed)
    _w = jnp.asarray

    def _rec_inputs():
        import jax
        import jax.numpy as jnp
        _gk = jax.random.key(seed)
        x = -0.0002117 + 1 * jax.random.normal(jax.random.fold_in(_gk, 1), (10000, 512), jnp.float32)
        _s = jax.random.randint(jax.random.fold_in(_gk, 2), (5000,), 0, 10000, jnp.int32)
        _d = jax.random.randint(jax.random.fold_in(_gk, 3), (5000,), 0, 10000, jnp.int32)
        _loop = jnp.arange(10000, dtype=jnp.int32)
        src = jnp.concatenate([_s, _d, _loop])
        dst = jnp.concatenate([_d, _s, _loop])
        _o = jnp.argsort(dst, stable=True)
        src = src[_o]
        dst = dst[_o]
        return (x, src, dst)
    x, src, dst = _rec_inputs()

    def _L0_gnn_setup():
        import jax, jax.numpy as jnp
        import numpy as np
        N_NODES = 50000
        N_EDGES = 25000
        IN_C = 512
        HID_C = 512

        def _sage_layer(x, src, dst, Wl, bl, Wr, a):
            n = x.shape[0]
            msg = x[src]
            agg = jax.ops.segment_sum(msg, dst, num_segments=n)
            deg = jax.ops.segment_sum(jnp.ones((src.shape[0],), x.dtype), dst, num_segments=n)
            agg = agg / jnp.maximum(deg, 1.0)[:, None]
            out = agg @ Wl + bl + x @ Wr
            return jnp.where(out >= 0, out, a * out)
        key = jax.random.key(seed)
        ks = jax.random.split(key, 16)
        x = jax.random.normal(ks[0], (N_NODES, IN_C), dtype=jnp.float32)
        edge_index = jax.random.randint(ks[1], (2, N_EDGES), 0, N_NODES, dtype=jnp.int64)
        inp = {'x': x, 'edge_index': edge_index}
        dims = [(IN_C, HID_C), (HID_C, HID_C), (HID_C, HID_C)]
        for i, (ci, co) in enumerate(dims):
            s = 1.0 / np.sqrt(ci)
            inp[f'Wl{i}'] = jax.random.uniform(ks[2 + 4 * i], (ci, co), jnp.float32, -s, s)
            inp[f'bl{i}'] = jax.random.uniform(ks[3 + 4 * i], (co,), jnp.float32, -s, s)
            inp[f'Wr{i}'] = jax.random.uniform(ks[4 + 4 * i], (ci, co), jnp.float32, -s, s)
            inp[f'a{i}'] = jnp.full((co,), 0.25, dtype=jnp.float32)
        return inp
    _L0_gnn_all = _L0_gnn_setup()
    _L0_gnn_in = {k: v for k, v in _L0_gnn_all.items() if k in ('Wl0', 'bl0', 'Wr0', 'a0', 'Wl1', 'bl1', 'Wr1', 'a1', 'Wl2', 'bl2', 'Wr2', 'a2')}
    del _L0_gnn_all

    def _L0_ffn_setup():
        import jax, jax.numpy as jnp
        import numpy as np
        B, T, D, F, E, K = (8, 1024, 512, 64, 8, 2)

        def _moe_forward(x, Wr, br, W1, b1, W2, b2):
            Bx, Tx, Dx = x.shape
            xf = x.reshape(-1, Dx)
            logits = xf @ Wr + br
            probs = jax.nn.softmax(logits, axis=-1)
            vals, idx = jax.lax.top_k(probs, K)
            cw = (jax.nn.one_hot(idx, E, dtype=x.dtype) * vals[..., None]).sum(axis=1)

            def body(acc, params):
                W1e, b1e, W2e, b2e, cwe = params
                h = jax.nn.relu(xf @ W1e + b1e)
                y = h @ W2e + b2e
                return (acc + cwe[:, None] * y, None)
            out, _ = jax.lax.scan(body, jnp.zeros_like(xf), (W1, b1, W2, b2, cw.T))
            return out.reshape(Bx, Tx, Dx)
        key = jax.random.key(seed)
        k0, k1, k2, k3 = jax.random.split(key, 4)
        s_d = 1.0 / np.sqrt(D)
        s_f = 1.0 / np.sqrt(F)
        return {'x': jax.random.normal(k0, (B, T, D), jnp.float32), 'Wr': jax.random.uniform(k1, (D, E), jnp.float32, -s_d, s_d), 'br': jnp.zeros((E,), jnp.float32), 'W1': jax.random.uniform(k2, (E, D, F), jnp.float32, -s_d, s_d), 'b1': jnp.zeros((E, F), jnp.float32), 'W2': jax.random.uniform(k3, (E, F, D), jnp.float32, -s_f, s_f), 'b2': jnp.zeros((E, D), jnp.float32)}
    _L0_ffn_all = _L0_ffn_setup()
    _L0_ffn_in = {k: v for k, v in _L0_ffn_all.items() if k in ('Wr', 'br', 'W1', 'b1', 'W2', 'b2')}
    del _L0_ffn_all
    return {'x': x, 'src': src, 'dst': dst, 'L0_gnn_Wl0': _L0_gnn_in['Wl0'], 'L0_gnn_bl0': _L0_gnn_in['bl0'], 'L0_gnn_Wr0': _L0_gnn_in['Wr0'], 'L0_gnn_a0': _L0_gnn_in['a0'], 'L0_gnn_Wl1': _L0_gnn_in['Wl1'], 'L0_gnn_bl1': _L0_gnn_in['bl1'], 'L0_gnn_Wr1': _L0_gnn_in['Wr1'], 'L0_gnn_a1': _L0_gnn_in['a1'], 'L0_gnn_Wl2': _L0_gnn_in['Wl2'], 'L0_gnn_bl2': _L0_gnn_in['bl2'], 'L0_gnn_Wr2': _L0_gnn_in['Wr2'], 'L0_gnn_a2': _L0_gnn_in['a2'], 'L0_ffn_Wr': _L0_ffn_in['Wr'], 'L0_ffn_br': _L0_ffn_in['br'], 'L0_ffn_W1': _L0_ffn_in['W1'], 'L0_ffn_b1': _L0_ffn_in['b1'], 'L0_ffn_W2': _L0_ffn_in['W2'], 'L0_ffn_b2': _L0_ffn_in['b2']}

def reference(x, src, dst, L0_gnn_Wl0, L0_gnn_bl0, L0_gnn_Wr0, L0_gnn_a0, L0_gnn_Wl1, L0_gnn_bl1, L0_gnn_Wr1, L0_gnn_a1, L0_gnn_Wl2, L0_gnn_bl2, L0_gnn_Wr2, L0_gnn_a2, L0_ffn_Wr, L0_ffn_br, L0_ffn_W1, L0_ffn_b1, L0_ffn_W2, L0_ffn_b2):
    import jax
    import jax.numpy as jnp

    def _L0_gnn_ref(x, edge_index, Wl0, bl0, Wr0, a0, Wl1, bl1, Wr1, a1, Wl2, bl2, Wr2, a2):
        import jax, jax.numpy as jnp
        import numpy as np
        N_NODES = 50000
        N_EDGES = 25000
        IN_C = 512
        HID_C = 512

        def _sage_layer(x, src, dst, Wl, bl, Wr, a):
            n = x.shape[0]
            msg = x[src]
            agg = jax.ops.segment_sum(msg, dst, num_segments=n)
            deg = jax.ops.segment_sum(jnp.ones((src.shape[0],), x.dtype), dst, num_segments=n)
            agg = agg / jnp.maximum(deg, 1.0)[:, None]
            out = agg @ Wl + bl + x @ Wr
            return jnp.where(out >= 0, out, a * out)
        src, dst = (edge_index[0], edge_index[1])
        x = _sage_layer(x, src, dst, Wl0, bl0, Wr0, a0)
        x = _sage_layer(x, src, dst, Wl1, bl1, Wr1, a1)
        x = _sage_layer(x, src, dst, Wl2, bl2, Wr2, a2)
        return x

    def _L0_ffn_ref(x, Wr, br, W1, b1, W2, b2):
        import jax, jax.numpy as jnp
        import numpy as np
        B, T, D, F, E, K = (8, 1024, 512, 64, 8, 2)

        def _moe_forward(x, Wr, br, W1, b1, W2, b2):
            Bx, Tx, Dx = x.shape
            xf = x.reshape(-1, Dx)
            logits = xf @ Wr + br
            probs = jax.nn.softmax(logits, axis=-1)
            vals, idx = jax.lax.top_k(probs, K)
            cw = (jax.nn.one_hot(idx, E, dtype=x.dtype) * vals[..., None]).sum(axis=1)

            def body(acc, params):
                W1e, b1e, W2e, b2e, cwe = params
                h = jax.nn.relu(xf @ W1e + b1e)
                y = h @ W2e + b2e
                return (acc + cwe[:, None] * y, None)
            out, _ = jax.lax.scan(body, jnp.zeros_like(xf), (W1, b1, W2, b2, cw.T))
            return out.reshape(Bx, Tx, Dx)
        return _moe_forward(x, Wr, br, W1, b1, W2, b2)
    edge_index = jnp.stack([src, dst])
    x = x + _L0_gnn_ref(_layernorm(x, axis=-1), edge_index, L0_gnn_Wl0, L0_gnn_bl0, L0_gnn_Wr0, L0_gnn_a0, L0_gnn_Wl1, L0_gnn_bl1, L0_gnn_Wr1, L0_gnn_a1, L0_gnn_Wl2, L0_gnn_bl2, L0_gnn_Wr2, L0_gnn_a2)
    x = x + _L0_ffn_ref(_layernorm(x, axis=-1)[None], L0_ffn_Wr, L0_ffn_br, L0_ffn_W1, L0_ffn_b1, L0_ffn_W2, L0_ffn_b2)[0]
    return x

_drawn_inputs = setup_inputs


def setup_inputs(seed=0):
    import zlib

    import numpy as np

    out = dict(_drawn_inputs(seed))
    spreads = {'L0_gnn_a0': (0.25, 0.6),
     'L0_gnn_a1': (0.25, 0.6),
     'L0_gnn_a2': (0.25, 0.6),
     'L0_ffn_br': (0.0, 0.1),
     'L0_ffn_b1': (0.0, 0.635),
     'L0_ffn_b2': (0.0, 0.1)}
    factors = {'L0_gnn_bl0': 7.775, 'L0_gnn_bl1': 4.666, 'L0_gnn_bl2': 2.689}
    for name, (base, spread) in spreads.items():
        noise = np.random.default_rng([zlib.crc32(name.encode()), seed]).standard_normal(out[name].shape)
        drawn = base * np.exp(spread * noise) if base else spread * noise
        out[name] = jnp.asarray(drawn.astype(out[name].dtype))
    for name, factor in factors.items():
        out[name] = (out[name] * factor).astype(out[name].dtype)
    return out
```

```python
from contextlib import ExitStack

import concourse.bass as bass
from concourse import mybir

ALU = mybir.AluOpType
ACT = mybir.ActivationFunctionType
AX = mybir.AxisListType
F32 = mybir.dt.float32
F32R = mybir.dt.float32r
BF16 = mybir.dt.bfloat16
I32 = mybir.dt.int32
U32 = mybir.dt.uint32

P = 128
EPS = 1e-5
FAR = 1 << 22


def at(i, c, ring):
    return i * ring + c, c % ring, i + c // ring


def build(nc, x, src, dst, Wl, bl, Wr, al, Wg, bg, W1, b1, W2, b2, out):
    N, D = x.shape
    E = src.shape[0]
    X = W1.shape[0]
    F = W1.shape[2]
    C = D // P
    LAYERS = len(Wl)
    NT = -(-N // P)
    ET = -(-E // P)
    ER = E - (ET - 1) * P
    NR = N - (NT - 1) * P
    PAIRS = NT // 2
    assert D == 512 and X * F == 512 and X == 8 and NT == 2 * PAIRS + 1 and ET == 4 * PAIRS + 1
    EB = ET - P
    ZERO = ET * P
    BLOCKS = [(0, P), (1, EB)]

    def uses(slot):
        return PAIRS + (slot == 0)

    y_d = nc.dram_tensor("y_rows", (NT * P, D), F32, kind="Internal").ap()
    s_d = nc.dram_tensor("sum_rows", (ET * P + 1, D), F32, kind="Internal").ap()

    with ExitStack() as ctx:
        def sb(name, shape, dt=F32):
            return ctx.enter_context(nc.sbuf_tensor(name, shape, dt))

        def pb(name, shape, dt=F32):
            return ctx.enter_context(nc.psum_tensor(name, shape, dt))

        def sem(name):
            return ctx.enter_context(nc.semaphore(name))

        def sems(name, n):
            return [sem(f"{name}{k}") for k in range(n)]

        res = sb("res", [P, NT, D])
        wy_at = nc.sbuf_base
        wy = sb("wy", [P, C, D])
        wz = sb("wz", [P, C, D])
        rows = sb("rows", [P, 4, D])
        outs = sb("outs", [P, 4, D])
        xTs = sb("xTs", [P, 2, C, P])
        hTs_at = nc.sbuf_base
        hTs = sb("hTs", [P, 2, C, P])
        bvec = sb("bvec", [P, D])
        avec = sb("avec", [P, D])
        b2s = sb("b2s", [X, D])
        ident = sb("ident", [P, P])
        iota = sb("iota", [P, P])
        lists = sb("lists", [P, 2 * ET])
        nodeI = sb("nodeI", [P, NT], I32)
        rdeg = sb("rdeg", [P, NT])
        ixe = sb("ixe", [P, 4], I32)
        ixn = sb("ixn", [P, 2], I32)
        ixf = sb("ixf", [P, 4], I32)
        wgs = sb("wgs", [P, C, X])
        bgs = sb("bgs", [P, X])
        half = sb("half", [P, 1])
        scrap = sb("scrap", [1, 1])
        st = sb("st", [P, 2, 12])
        sm = sb("sm", [P, 2, 4 * X])
        LG, PR, TOP, CW = (X * k for k in range(4))
        smi = sb("smi", [P, 8], U32)
        op = sb("op", [P, 2, 8])
        LO, HI, DST, START, HEAD, BEGUN, NEXT, PREV = range(8)

        hTs0 = hTs[:, 0].rearrange("p c n -> p (c n)")
        hTs1 = hTs[:, 1].rearrange("p c n -> p (c n)")
        srcT = lists[:, 0:ET].bitcast(I32)
        headT = lists[:, ET:2 * ET]
        cwT = lists[0:X, 0:2 * P].rearrange("e (s p) -> e s p", s=2)
        parts = nc.alloc_sbuf_tensor_at("parts", [P, 2, 2, D], F32R, offset=wy_at)
        sel = nc.alloc_sbuf_tensor_at("sel", [P, 4, P], F32R, offset=hTs_at)
        lower, ones, first = (hTs[:, 0, k, :] for k in range(3))
        onehot = hTs1.bitcast(BF16).rearrange("p (g n) -> p g n", g=4)
        mendM = hTs1[:, 0:2 * ET].rearrange("p (b t) -> p b t", b=2)
        openlo = [hTs1[:, 320:320 + P], outs[:, 3, 320:320 + P]]
        loT = outs[:, 3, 0:ET]
        hiT = outs[:, 3, ET:2 * ET]
        counts, colsum, starts, work = (outs[:, 2, 80 * k:80 * k + NT] for k in range(4))
        dstT = outs[:, 2, 320:320 + ET]

        def tmp(k, n=P):
            return res[:, NT - 8 + k // 4, (k % 4) * P:(k % 4) * P + n]

        ints = {"src": (0, 1), "dst": (2, 3), "lo": (4, 5), "hi": (6, 7)}
        flts = {"src": (8, 9), "lo": (10, 11), "hi": (12, 13), "head": (14, 15), "dst": (16, 17), "val": (18, 19)}
        zeros = tmp(24, D)

        def int_rows(name, b):
            return tmp(ints[name][b]).bitcast(I32)

        def flt_rows(name, b):
            return tmp(flts[name][b])

        psT = [pb(f"psT{s}", [P, D]) for s in range(2)]
        psY = [pb(f"psY{s}", [P, D]) for s in range(2)]
        psS = [pb(f"psS{s}", [P, D]) for s in range(2)]
        psH = pb("psH", [P, D])
        psM = pb("psM", [P, D])

        ids_pad = sem("ids_pad")
        ids_in = sem("ids_in")
        const_set = sem("const_set")
        small_in = sem("small_in")
        zero_set = sem("zero_set")
        zero_st = sem("zero_st")
        rows_set = sem("rows_set")
        lists_ps = sem("lists_ps")
        lists_set = sem("lists_set")
        plan_in = sem("plan_in")
        plan_ps = sem("plan_ps")
        plan_rp = sem("plan_rp")
        plan_hf = sem("plan_hf")
        plan_done = sem("plan_done")
        wy_in = sem("wy_in")
        wz_in = sem("wz_in")
        bvec_in = sem("bvec_in")
        avec_in = sem("avec_in")
        x_in = sems("x_in", 2)
        xe_in = sems("xe_in", 2)
        ix_n = sems("ix_n", 2)
        node_in = sems("node_in", 2)
        vchain = sem("vchain")
        xn_ready = sems("xn_ready", 2)
        xT_ps = sems("xT_ps", 2)
        xT_sb = sems("xT_sb", 2)
        xT_kept = sems("xT_kept", 2)
        y_ps = sems("y_ps", 2)
        y_sb = sems("y_sb", 2)
        y_st = sems("y_st", 2)
        var_in = sems("var_in", 2)
        rstd_in = sems("rstd_in", 2)
        oh_set = sems("oh_set", 4)
        oh_used = sems("oh_used", 4)
        ix_e = sems("ix_e", 4)
        edge_in = sems("edge_in", 4)
        hi_set = sems("hi_set", 4)
        lo_set = sems("lo_set", 4)
        sel_set = sems("sel_set", 4)
        seg_ps = sems("seg_ps", 4)
        seg_sb = sems("seg_sb", 4)
        seg_st = sems("seg_st", 4)
        xT_back = sems("xT_back", 2)
        z_ps = sems("z_ps", 2)
        z_sb = sems("z_sb", 2)
        mend_in = sem("mend_in")
        mend_g = sem("mend_g")
        mend_ps = sem("mend_ps")
        mend_add = sem("mend_add")
        mend_st = sem("mend_st")
        lg_ps = sems("lg_ps", 2)
        lg_sb = sems("lg_sb", 2)
        p_sb = sems("p_sb", 2)
        cw_set = sems("cw_set", 2)
        hg_sb = sems("hg_sb", 2)
        cw_ps = sems("cw_ps", 2)
        cw_sb = sems("cw_sb", 2)
        hT_ps = sems("hT_ps", 2)
        hT_sb = sems("hT_sb", 2)
        o_ps = sems("o_ps", 2)
        o_sb = sems("o_sb", 2)
        o_st = sems("o_st", 2)

        block = ctx.enter_context(nc.Block())

        def all_turns(eng, signals, rounds, step=1):
            for slot, s in enumerate(signals):
                eng.wait_ge(s, rounds * uses(slot) * step)

        def turns(eng, n, fresh):
            if fresh:
                yield 0
            with eng.Fori(1 if fresh else 0, n) as i:
                yield i

        def each_pair(eng, step, fresh):
            for i in turns(eng, PAIRS, fresh):
                for c in range(2):
                    step(i, c)
            step(PAIRS, 0)

        def each_four(eng, step, fresh):
            for i in turns(eng, PAIRS, fresh):
                for c in range(4):
                    step(i, c)
            step(PAIRS, 0)

        def rows_of(t, n=P):
            return slice(t * P, t * P + n) if isinstance(t, int) else bass.ds(t * P, n)

        def kept(t, n=P):
            return res[0:n, t, :] if isinstance(t, int) else res[0:n, bass.ds(t, 1), :].rearrange("p a d -> p (a d)")

        def col(table, t):
            return table[:, t:t + 1] if isinstance(t, int) else table[:, bass.ds(t, 1)]

        def load_x(eng, i, c, ring, rounds, signal):
            t, s, n = at(i, c, 2)
            eng.wait_ge(xn_ready[s], rounds * uses(s) + n)
            r = NR if isinstance(t, int) and t == NT - 1 else P
            eng.dma_start(ring[0:r, s, :], x[rows_of(t, r)]).then_inc(signal[s], 16)

        @block.sync
        def _(sp):
            def load_w(buf, w, signal):
                sp.dma_start(buf[:, :, :], w.rearrange("(c p) n -> p c n", p=P)).then_inc(signal, 16)

            def load_row(buf, v, signal):
                sp.dma_start(buf[:, :], v.partition_broadcast(P)).then_inc(signal, 16)

            def store_y(i, c, k):
                t, s, n = at(i, c, 2)
                sp.wait_ge(y_sb[s], k * uses(s) + n + 1)
                sp.dma_start(y_d[rows_of(t)], outs[:, s, :]).then_inc(y_st[s], 16)

            sp.wait_ge(ids_pad, 2)
            for name, v in (("src", src), ("dst", dst)):
                sp.dma_start(int_rows(name, 0), v[0:P * P].rearrange("(t p) -> t p", p=P)).then_inc(ids_in, 16)
                sp.dma_start(int_rows(name, 1)[0:EB - 1], v[P * P:E - ER].rearrange("(t p) -> t p", p=P))\
                  .then_inc(ids_in, 16)
                sp.dma_start(int_rows(name, 1)[EB - 1:EB, 0:ER], v[E - ER:E].rearrange("(t p) -> t p", p=ER))\
                  .then_inc(ids_in, 16)
            load_w(wy, Wl[0], wy_in)
            sp.wait_ge(zero_set, 1)
            sp.dma_start(s_d[ZERO:ZERO + 1], zeros[0:1, :]).then_inc(zero_st, 16)
            load_w(wz, Wr[0], wz_in)
            load_row(bvec, bl[0], bvec_in)
            load_row(avec, al[0], avec_in)
            load_row(bgs, bg, small_in)
            sp.dma_start(wgs[:, :, :], Wg.rearrange("(c p) n -> p c n", p=P)).then_inc(small_in, 16)
            sp.dma_start(b2s[:, :], b2).then_inc(small_in, 16)
            each_pair(sp, lambda i, c: store_y(i, c, 0), True)

            def store_seg(i, c, l):
                t, g, n = at(i, c, 4)
                sp.wait_ge(seg_sb[g], l * uses(g) + n + 1)
                sp.dma_start(s_d[rows_of(t)], outs[:, g, :]).then_inc(seg_st[g], 16)

            for l in range(LAYERS):
                if l > 0:
                    all_turns(sp, xn_ready, l + 1)
                    load_row(avec, al[l], avec_in)
                each_four(sp, lambda i, c: store_seg(i, c, l), l == 0)
                for g in range(4):
                    sp.wait_ge(seg_ps[g], (l + 1) * uses(g))
                if l + 1 < LAYERS:
                    load_w(wy, Wl[l + 1], wy_in)
                else:
                    for e in range(X):
                        sp.dma_start(wy[:, :, e * F:(e + 1) * F], W1[e].rearrange("(c p) f -> p c f", p=P))\
                          .then_inc(wy_in, 16)
                for g in range(4):
                    sp.wait_ge(seg_st[g], 16 * (l + 1) * uses(g))
                starts_d = s_d[0:ET * P].rearrange("(t p) d -> t p d", p=P)[:, 0, :]
                for b, r in BLOCKS:
                    sp.dma_start(rows[0:r, b, :], starts_d[b * P:b * P + r]).then_inc(mend_in, 16)
                all_turns(sp, z_sb, l + 1)
                if l + 1 < LAYERS:
                    load_w(wz, Wr[l + 1], wz_in)
                    load_row(bvec, bl[l + 1], bvec_in)
                    each_pair(sp, lambda i, c: store_y(i, c, l + 1), False)
                else:
                    load_w(wz, W2.rearrange("e f d -> (e f) d"), wz_in)
                    load_row(bvec, b1.rearrange("e f -> (e f)"), bvec_in)

            def store_out(i, c, r=P):
                t, s, n = at(i, c, 2)
                sp.wait_ge(o_sb[s], n + 1)
                sp.dma_start(out[rows_of(t, r)], kept(t, r)).then_inc(o_st[s], 16)

            for c in range(4):
                load_x(sp, 0, c, outs, LAYERS, xe_in)
            for i in turns(sp, PAIRS - 2, True):
                for c in range(2):
                    load_x(sp, i, c + 4, outs, LAYERS, xe_in)
                    store_out(i, c)
            load_x(sp, PAIRS, 0, outs, LAYERS, xe_in)
            for c in range(4):
                store_out(PAIRS - 2, c)
            store_out(PAIRS, 0, NR)
            all_turns(sp, o_st, 1, 16)
            sp.wait_ge(zero_st, 16)

        @block.gpsimd
        def _(pool):
            pool.memset(int_rows("src", 1), 0).then_inc(ids_pad, 1)
            pool.memset(int_rows("dst", 1), -1).then_inc(ids_pad, 1)
            pool.iota(iota[:, :], pattern=[[1, P]], base=0, channel_multiplier=0,
                      allow_small_or_imprecise_dtypes=True).then_inc(const_set, 1)
            pool.memset(ident[:, :], 0.0).then_inc(const_set, 1)
            pool.memset(hTs0[:, 0:2 * P], 1.0).then_inc(const_set, 1)
            pool.memset(hTs0[:, 2 * P:3 * P], 0.0).then_inc(const_set, 1)
            pool.memset(zeros[0:1, :], 0.0).then_inc(zero_set, 1)
            pool.wait_ge(const_set, 4)
            pool.affine_select(out=ident[:, :], in_=ident[:, :], compare_op=ALU.not_equal, fill=1.0, base=0,
                               pattern=[[-1, P]], channel_multiplier=1).then_inc(const_set, 1)
            pool.affine_select(out=lower, in_=lower, compare_op=ALU.is_gt, fill=0.0, base=0,
                               pattern=[[1, P]], channel_multiplier=-1).then_inc(const_set, 1)
            pool.memset(first[0:1, :], 1.0).then_inc(const_set, 1)
            for b, r in BLOCKS:
                pool.iota(op[:, b, START:START + 1], pattern=[[0, 1]], base=b * P * P, channel_multiplier=P,
                          allow_small_or_imprecise_dtypes=True).then_inc(const_set, 1)

            pool.memset(half[:, :], -0.5).then_inc(const_set, 1)
            pool.wait_ge(const_set, 10)

            def rstd(i, c, k):
                t, s, n = at(i, c, 2)
                pool.wait_ge(var_in[s], k * uses(s) + n + 1)
                pool.tensor_tensor(st[:, s, 8:9], st[:, s, 7:8], half[:, :], ALU.pow).then_inc(rstd_in[s], 1)

            load_x(pool, 0, 0, rows, 0, x_in)
            load_x(pool, 0, 1, rows, 0, x_in)
            for i in turns(pool, PAIRS - 1, True):
                for c in range(2):
                    rstd(i, c, 0)
                    load_x(pool, i, c + 2, rows, 0, x_in)
            rstd(PAIRS - 1, 0, 0)
            load_x(pool, PAIRS, 0, rows, 0, x_in)
            rstd(PAIRS - 1, 1, 0)
            rstd(PAIRS, 0, 0)

            def gather_edge(i, c, l):
                t, g, n = at(i, c, 4)
                used = l * uses(g) + n
                pool.wait_ge(lo_set[g], used)
                pool.tensor_copy(ixe[:, g:g + 1], col(srcT, t)).then_inc(ix_e[g], 1)
                pool.wait_ge(ix_e[g], used + 1)
                pool.indirect_dma_start(out=rows[:, g, :], out_offset=None, in_=y_d,
                                        in_offset=bass.IndirectOffsetOnAxis(ap=ixe[:, g:g + 1], axis=0),
                                        bounds_check=i + (NT * P - 1 + c)).then_inc(edge_in[g], 16)

            def gather_node(i, c, l):
                t, s, n = at(i, c, 2)
                used = l * uses(s) + n
                pool.wait_ge(xn_ready[s], uses(s) + used)
                pool.tensor_copy(ixn[:, s:s + 1], col(nodeI, t)).then_inc(ix_n[s], 1)
                pool.wait_ge(ix_n[s], used + 1)
                pool.indirect_dma_start(out=rows[:, s, :], out_offset=None, in_=s_d,
                                        in_offset=bass.IndirectOffsetOnAxis(ap=ixn[:, s:s + 1], axis=0),
                                        bounds_check=i + (ZERO + c)).then_inc(node_in[s], 16)

            for l in range(LAYERS):
                if l == 0:
                    pool.wait_ge(lists_set, 1)
                all_turns(pool, y_st, l + 1, 16)
                each_four(pool, lambda i, c: gather_edge(i, c, l), l == 0)
                for g in range(4):
                    pool.wait_ge(seg_st[g], 16 * (l + 1) * uses(g))
                if l == 0:
                    pool.wait_ge(plan_done, 1)
                    pool.wait_ge(zero_st, 16)
                for b, r in BLOCKS:
                    pool.indirect_dma_start(out=rows[0:r, 2 + b, :], out_offset=None, in_=s_d,
                                            in_offset=bass.IndirectOffsetOnAxis(ap=ixf[0:r, b:b + 1], axis=0),
                                            bounds_check=ZERO).then_inc(mend_g, 16)
                pool.wait_ge(mend_in, 32 * (l + 1))
                pool.wait_ge(mend_g, 32 * (l + 1))
                for b, r in BLOCKS:
                    pool.wait_ge(mend_add, 2 * l + b + 1)
                    pool.indirect_dma_start(out=s_d, out_offset=bass.IndirectOffsetOnAxis(
                                                ap=ixf[0:r, 2 + b:3 + b], axis=0),
                                            in_=rows[0:r, 2 + b, :], in_offset=None,
                                            bounds_check=ZERO, oob_is_err=False).then_inc(mend_st, 16)
                pool.wait_ge(mend_st, 32 * (l + 1))
                if l + 1 < LAYERS:
                    each_pair(pool, lambda i, c: gather_node(i, c, l), l == 0)
            gather_node(0, 0, LAYERS - 1)
            gather_node(0, 1, LAYERS - 1)
            for i in turns(pool, PAIRS - 1, True):
                for c in range(2):
                    rstd(i, c, 1)
                    gather_node(i, c + 2, LAYERS - 1)
            rstd(PAIRS - 1, 0, 1)
            gather_node(PAIRS, 0, LAYERS - 1)
            rstd(PAIRS - 1, 1, 1)
            rstd(PAIRS, 0, 1)

        @block.tensor
        def _(pe):
            def transposes(dest, tile, signal=None):
                for c in range(C):
                    mm = pe.transpose(dest[:, c * P:(c + 1) * P], tile[:, c * P:(c + 1) * P], ident[:, :])
                if signal is not None:
                    mm.then_inc(signal, 1)

            def product(dest, xT, w, signal=None, last=True):
                for c in range(C):
                    mm = pe.matmul(dest, xT[:, c, :], w[:, c, :], start=(c == 0), stop=(last and c == C - 1))
                if signal is not None:
                    mm.then_inc(signal, 1)

            pe.wait_ge(const_set, 9)
            pe.wait_ge(rows_set, 1)
            for b, r in BLOCKS:
                for k, name in enumerate(("src", "lo", "hi", "head")):
                    mm = pe.transpose(psS[b][:, k * P:k * P + r], flt_rows(name, b)[0:r, :], ident[0:r, 0:r])
                mm.then_inc(lists_ps, 1)

            def x_transpose(i, c, k):
                t, s, n = at(i, c, 2)
                pe.wait_ge(xn_ready[s], k * uses(s) + n + 1)
                pe.wait_ge(xT_kept[s], k * uses(s) + n)
                transposes(psT[s], rows[:, 2 + s, :], xT_ps[s])

            def y_product(i, c, k):
                t, s, n = at(i, c, 2)
                pe.wait_ge(xT_sb[s], k * uses(s) + n + 1)
                pe.wait_ge(y_sb[s], k * uses(s) + n)
                product(psY[s][:, :], xTs[:, s], wy, y_ps[s])

            def count(i, c, start=False):
                t, g, n = at(i, c, 4)
                pe.wait_ge(oh_set[g], 2 * (n + 1))
                pe.matmul(psH[:, 0:NT], onehot[:, g, 0:P], onehot[:, g, P:P + NT], start=start, stop=True,
                          skip_group_check=True).then_inc(oh_used[g], 1)

            def dense(k):
                pe.wait_ge(wy_in, 16 * (k + 1))
                if k > 0:
                    all_turns(pe, z_sb, k)
                x_transpose(0, 0, k)
                if k == 0:
                    count(0, 0, True)
                for i in turns(pe, PAIRS, k == 0):
                    for c in range(2):
                        x_transpose(i, c + 1, k)
                        y_product(i, c, k)
                        if k == 0:
                            count(i, 2 * c + 1)
                            count(i, 2 * c + 2)
                y_product(PAIRS, 0, k)

            def make_plan():
                pe.wait_ge(plan_in, 1)
                pe.matmul(psM[:, 0:NT], lower, counts, start=True, stop=True)
                pe.matmul(psM[:, P:P + NT], ones, counts, start=True, stop=True)
                pe.matmul(psM[:, 2 * P:2 * P + ET], first, dstT, start=True, stop=True)
                for b, r in BLOCKS:
                    mm = pe.transpose(psH[:, (1 + b) * P:(1 + b) * P + r], openlo[b][0:r, :], ident[0:r, 0:r])
                mm.then_inc(plan_ps, 1)
                pe.wait_ge(plan_rp, 1)
                for b, r in BLOCKS:
                    mm = pe.matmul(psS[b][0:r, 0:NT], openlo[b][:, 0:r], starts, start=True, stop=True)
                mm.then_inc(plan_hf, 1)

            def z_product(i, c, l):
                t, s, n = at(i, c, 2)
                pe.wait_ge(xT_back[s], l * uses(s) + n + 1)
                pe.wait_ge(z_sb[s], l * uses(s) + n)
                product(psY[s][:, :], xTs[:, s], wz, z_ps[s])

            def segment_sum(i, c, l):
                t, g, n = at(i, c, 4)
                used = l * uses(g) + n
                before = (g + 2) % 4
                pe.wait_ge(seg_sb[before], l * uses(before) + n + (g >= 2))
                pe.wait_ge(sel_set[g], used + 1)
                pe.wait_ge(hi_set[g], used + 1)
                pe.wait_ge(lo_set[g], used + 1)
                pe.matmul(psS[g % 2][:, :], sel[:, g, :], parts[:, g % 2, 0, :], start=True, stop=False)
                pe.matmul(psS[g % 2][:, :], sel[:, g, :], parts[:, g % 2, 1, :], start=False, stop=True)\
                  .then_inc(seg_ps[g], 1)

            for l in range(LAYERS):
                dense(l)
                if l == 0:
                    make_plan()
                all_turns(pe, y_sb, l + 1)
                pe.wait_ge(wz_in, 16 * (l + 1))
                for i in turns(pe, PAIRS, l == 0):
                    for c in range(2):
                        z_product(i, c, l)
                        segment_sum(i, 2 * c, l)
                        segment_sum(i, 2 * c + 1, l)
                z_product(PAIRS, 0, l)
                segment_sum(PAIRS, 0, l)
                for g in range(4):
                    pe.wait_ge(seg_sb[g], (l + 1) * uses(g))
                pe.wait_ge(mend_in, 32 * (l + 1))
                for b, r in BLOCKS:
                    for kb, kr in BLOCKS:
                        mm = pe.matmul(psS[b][0:r, :], mendM[0:kr, kb, b * P:b * P + r], rows[0:kr, kb, :],
                                       start=(kb == 0), stop=(kb == 1))
                    mm.then_inc(mend_ps, 1)

            def x_turn(i, c):
                t, s, n = at(i, c, 2)
                pe.wait_ge(xn_ready[s], LAYERS * uses(s) + n + 1)
                pe.wait_ge(xT_sb[s], LAYERS * uses(s) + n)
                transposes(psT[s], rows[:, 2 + s, :], xT_ps[s])

            def router_and_up(i, c, first=False):
                t, s, n = at(i, c, 2)
                pe.wait_ge(xT_sb[s], LAYERS * uses(s) + n + 1)
                _, so, no = at(i, c - 1, 2)
                if not first:
                    pe.wait_ge(cw_sb[so], no + 1)
                product(psM[:, 0:X], xTs[:, s], wgs, lg_ps[s])
                pe.wait_ge(hg_sb[s], n)
                product(psY[s][:, :], xTs[:, s], wy, y_ps[s])

            def hidden_turn(i, c):
                t, s, n = at(i, c, 2)
                pe.wait_ge(cw_set[s], n + 1)
                pe.transpose(psM[0:X, P:2 * P], sm[:, s, CW:CW + X], ident[:, :]).then_inc(cw_ps[s], 1)
                pe.wait_ge(hg_sb[s], n + 1)
                pe.wait_ge(hT_sb[s], n)
                transposes(psS[s], outs[:, 2 + s, :], hT_ps[s])

            def down(i, c, first=False):
                t, s, n = at(i, c, 2)
                _, so, no = at(i, c - 1, 2)
                if not first:
                    pe.wait_ge(o_sb[so], no + 1)
                pe.wait_ge(hT_sb[s], n + 1)
                pe.wait_ge(cw_sb[s], n + 1)
                product(psH[:, :], hTs[:, s], wz, last=False)
                pe.matmul(psH[:, :], cwT[:, s, :], b2s[:, :], start=False, stop=True).then_inc(o_ps[s], 1)

            pe.wait_ge(wy_in, 16 * (LAYERS + X))
            pe.wait_ge(wz_in, 16 * (LAYERS + 1))
            pe.wait_ge(small_in, 48)
            x_turn(0, 0)
            x_turn(0, 1)
            router_and_up(0, 0, True)
            hidden_turn(0, 0)
            x_turn(0, 2)
            router_and_up(0, 1)
            down(0, 0, True)
            for i in turns(pe, PAIRS - 1, True):
                for c in (1, 2):
                    hidden_turn(i, c)
                    x_turn(i, c + 2)
                    router_and_up(i, c + 1)
                    down(i, c)
            hidden_turn(PAIRS - 1, 1)
            router_and_up(PAIRS, 0)
            down(PAIRS - 1, 1)
            hidden_turn(PAIRS, 0)
            down(PAIRS, 0)

        @block.scalar
        def _(act):
            def copy(o, i_, signal):
                act.activation(o, i_, ACT.Copy).then_inc(signal, 1)

            def keep_xT(i, c, k):
                t, s, n = at(i, c, 2)
                act.wait_ge(xT_ps[s], k * uses(s) + n + 1)
                act.wait_ge(y_ps[s], k * uses(s) + n)
                copy(xTs[:, s].rearrange("p c n -> p (c n)"), psT[s][:, :], xT_sb[s])
                copy(kept(t), psT[s][:, :], xT_kept[s])

            def take_y(i, c, k):
                t, s, n = at(i, c, 2)
                act.wait_ge(y_ps[s], k * uses(s) + n + 1)
                act.wait_ge(y_st[s], 16 * (k * uses(s) + n))
                copy(outs[:, s, :], psY[s][:, :], y_sb[s])

            def give_xT(i, c, l):
                t, s, n = at(i, c, 2)
                act.wait_ge(z_ps[s], l * uses(s) + n)
                copy(xTs[:, s].rearrange("p c n -> p (c n)"), kept(t), xT_back[s])

            def high(i, c, l):
                t, g, n = at(i, c, 4)
                before = (g + 2) % 4
                act.wait_ge(edge_in[g], 16 * (l * uses(g) + n + 1))
                act.wait_ge(seg_ps[before], l * uses(before) + n + (g >= 2))
                copy(parts[:, g % 2, 0, :], rows[:, g, :], hi_set[g])

            def take_sums(i, c, l):
                t, g, n = at(i, c, 4)
                act.wait_ge(seg_ps[g], l * uses(g) + n + 1)
                act.wait_ge(seg_st[g], 16 * (l * uses(g) + n))
                copy(outs[:, g, :], psS[g % 2][:, :], seg_sb[g])

            for l in range(LAYERS):
                if l > 0:
                    for g in range(4):
                        act.wait_ge(seg_st[g], 16 * l * uses(g))
                    all_turns(act, z_ps, l)
                keep_xT(0, 0, l)
                for i in turns(act, PAIRS, l == 0):
                    for c in range(2):
                        keep_xT(i, c + 1, l)
                        take_y(i, c, l)
                take_y(PAIRS, 0, l)
                all_turns(act, xT_kept, l + 1)
                all_turns(act, y_st, l + 1, 16)
                give_xT(0, 0, l)
                high(0, 0, l)
                high(0, 1, l)
                for i in turns(act, PAIRS - 1, l == 0):
                    for c in range(2):
                        give_xT(i, c + 1, l)
                        for e in (2 * c, 2 * c + 1):
                            take_sums(i, e, l)
                            high(i, e + 2, l)
                give_xT(PAIRS - 1, 1, l)
                take_sums(PAIRS - 1, 0, l)
                high(PAIRS - 1, 2, l)
                take_sums(PAIRS - 1, 1, l)
                high(PAIRS - 1, 3, l)
                give_xT(PAIRS, 0, l)
                take_sums(PAIRS - 1, 2, l)
                high(PAIRS, 0, l)
                take_sums(PAIRS - 1, 3, l)
                take_sums(PAIRS, 0, l)

            def take_xT(i, c):
                t, s, n = at(i, c, 2)
                act.wait_ge(xT_ps[s], LAYERS * uses(s) + n + 1)
                act.wait_ge(y_ps[s], LAYERS * uses(s) + n)
                copy(xTs[:, s].rearrange("p c n -> p (c n)"), psT[s][:, :], xT_sb[s])

            def exps(i, c):
                t, s, n = at(i, c, 2)
                act.wait_ge(lg_sb[s], n + 1)
                act.activation(sm[:, s, PR:PR + X], sm[:, s, LG:LG + X], ACT.Exp, bias=st[:, s, 9:10],
                               accum_out=st[:, s, 10:11]).then_inc(p_sb[s], 1)

            def take_hT(i, c):
                t, s, n = at(i, c, 2)
                act.wait_ge(o_ps[s], n)
                act.wait_ge(cw_ps[s], n + 1)
                copy(cwT[:, s, :], psM[0:X, P:2 * P], cw_sb[s])
                act.wait_ge(hT_ps[s], n + 1)
                copy(hTs[:, s].rearrange("p c n -> p (c n)"), psS[s][:, :], hT_sb[s])

            all_turns(act, z_ps, LAYERS)
            act.wait_ge(mend_ps, 2 * LAYERS)
            take_xT(0, 0)
            take_xT(0, 1)
            exps(0, 0)
            take_hT(0, 0)
            take_xT(0, 2)
            exps(0, 1)
            for i in turns(act, PAIRS - 1, True):
                for c in (1, 2):
                    take_hT(i, c)
                    take_xT(i, c + 2)
                    exps(i, c + 1)
            take_hT(PAIRS - 1, 1)
            exps(PAIRS, 0)
            take_hT(PAIRS, 0)

        @block.vector
        def _(dve):
            done = [0]

            def link(ins):
                done[0] += 1
                ins.then_inc(vchain, 1)
                dve.wait_ge(vchain, done[0])

            def linker(tile, per):
                k = [0]
                base = done[0]

                def one(ins):
                    k[0] += 1
                    ins.then_inc(vchain, 1)
                    dve.wait_ge(vchain, tile * per + (base + k[0]))
                    assert k[0] <= per
                return one

            def copy(o, i_):
                return dve.tensor_copy(o, i_)

            dve.wait_ge(ids_in, 96)
            dve.wait_ge(const_set, 9)
            for b, r in BLOCKS:
                dve.tensor_scalar(int_rows("lo", b)[0:r], int_rows("dst", b)[0:r], P - 1, None,
                                  ALU.bitwise_and).then_inc(vchain, 1)
                dve.tensor_scalar(int_rows("hi", b)[0:r], int_rows("dst", b)[0:r], 7, None,
                                  ALU.arith_shift_right).then_inc(vchain, 1)
                dve.tensor_copy(flt_rows("dst", b)[0:r], int_rows("dst", b)[0:r]).then_inc(vchain, 1)
                dve.tensor_copy(flt_rows("src", b)[0:r], int_rows("src", b)[0:r]).then_inc(vchain, 1)
            done[0] += 8
            dve.wait_ge(vchain, done[0])
            for b, r in BLOCKS:
                val, dstf = flt_rows("val", b), flt_rows("dst", b)
                dve.tensor_copy(flt_rows("lo", b)[0:r], int_rows("lo", b)[0:r]).then_inc(vchain, 1)
                dve.tensor_copy(flt_rows("hi", b)[0:r], int_rows("hi", b)[0:r]).then_inc(vchain, 1)
                dve.memset(val[0:r, 0:1], 0.0).then_inc(vchain, 1)
                dve.tensor_copy(op[0:r, b, DST:DST + 1], dstf[0:r, 0:1]).then_inc(vchain, 1)
                dve.tensor_tensor(val[0:r, 1:P], dstf[0:r, 1:P], dstf[0:r, 0:P - 1], ALU.not_equal)\
                   .then_inc(vchain, 1)
            done[0] += 10
            dve.wait_ge(vchain, done[0])
            for b, r in BLOCKS:
                val = flt_rows("val", b)
                dve.tensor_copy(op[0:r, b, LO:LO + 1], flt_rows("lo", b)[0:r, 0:1]).then_inc(vchain, 1)
                dve.tensor_copy(op[0:r, b, HI:HI + 1], flt_rows("hi", b)[0:r, 0:1]).then_inc(vchain, 1)
                dve.tensor_tensor(val[0:r, 1:P], val[0:r, 1:P], iota[0:r, 1:P], ALU.mult).then_inc(vchain, 1)
            done[0] += 6
            dve.wait_ge(vchain, done[0])
            for b, r in BLOCKS:
                val = flt_rows("val", b)
                link(dve.tensor_tensor_scan(flt_rows("head", b)[0:r], val[0:r], val[0:r], 0.0,
                                            ALU.max, ALU.max))
            dve.sem_inc(rows_set, 1)
            dve.wait_ge(lists_ps, 2)
            for b, r in BLOCKS:
                for k, table in enumerate((srcT[:, :], loT, hiT, headT[:, :])):
                    dve.tensor_copy(table[:, b * P:b * P + r], psS[b][:, k * P:k * P + r]).then_inc(vchain, 1)
            done[0] += 8
            dve.wait_ge(vchain, done[0])
            dve.sem_inc(lists_set, 1)

            def carry():
                dve.memset(scrap[:, :], 0.0)

            def moments(s, node_rows, one):
                carry()
                one(dve.bn_stats(st[:, s, 0:6], node_rows))
                carry()
                one(dve.bn_aggr(st[:, s, 6:8], st[:, s, 0:6]))
                dve.tensor_scalar(st[:, s, 7:8], st[:, s, 7:8], EPS, None, ALU.add).then_inc(var_in[s], 1)

            def normed(i, c, k, node_rows):
                t, s, n = at(i, c, 2)
                dve.wait_ge(rstd_in[s], k * uses(s) + n + 1)
                dve.tensor_scalar(rows[:, 2 + s, :], node_rows, st[:, s, 6:7], st[:, s, 8:9],
                                  ALU.subtract, ALU.mult).then_inc(xn_ready[s], 1)

            def norm_x(i, c):
                t, s, n = at(i, c, 2)
                dve.wait_ge(x_in[s], 16 * (n + 1))
                moments(s, rows[:, s, :], linker(t, 2))

            def norm_x_end(i, c):
                t, s, n = at(i, c, 2)
                dve.wait_ge(xT_ps[s], n)
                normed(i, c, 0, rows[:, s, :])

            def one_hot(i, c):
                t, g, n = at(i, c, 4)
                dve.wait_ge(oh_used[g], n)
                dve.tensor_scalar(onehot[:, g, 0:P], iota[:, :], col(loT, t), None, ALU.is_equal)\
                   .then_inc(oh_set[g], 1)
                dve.tensor_scalar(onehot[:, g, P:P + NT], iota[:, 0:NT], col(hiT, t), None, ALU.is_equal)\
                   .then_inc(oh_set[g], 1)

            norm_x(0, 0)
            for i in turns(dve, PAIRS, True):
                for c in range(2):
                    norm_x_end(i, c)
                    one_hot(i, 2 * c)
                    one_hot(i, 2 * c + 1)
                    norm_x(i, c + 1)
            norm_x_end(PAIRS, 0)
            one_hot(PAIRS, 0)
            done[0] += 2 * NT

            def make_plan():
                for g in range(4):
                    dve.wait_ge(oh_used[g], uses(g))
                link(copy(counts, psH[:, 0:NT]))
                link(dve.tensor_scalar(rdeg[:, :], counts, 1.0, None, ALU.max))
                link(dve.reciprocal(rdeg[:, :], rdeg[:, :]))
                link(dve.scalar_tensor_tensor(dstT, hiT, float(P), loT, ALU.mult, ALU.add))
                for b, r in BLOCKS:
                    link(dve.tensor_scalar(openlo[b][0:r, :], iota[0:r, :], op[0:r, b, LO:LO + 1], None,
                                           ALU.is_equal))
                dve.sem_inc(plan_in, 1)
                dve.wait_ge(plan_ps, 1)
                link(copy(colsum, psM[:, P:P + NT]))
                link(dve.tensor_tensor_scan(work, ones[:, 0:NT], colsum, 0.0, ALU.mult, ALU.add))
                link(dve.tensor_tensor(work, work, colsum, ALU.subtract))
                link(dve.tensor_tensor(starts, work, psM[:, 0:NT], ALU.add))
                for b, r in BLOCKS:
                    link(copy(openlo[b][:, 0:r], psH[:, (1 + b) * P:(1 + b) * P + r]))
                dve.sem_inc(plan_rp, 1)
                link(dve.tensor_scalar(work, counts, 0.0, None, ALU.is_gt))
                link(dve.scalar_tensor_tensor(work, starts, float(-ZERO), work, ALU.add, ALU.mult))
                link(dve.tensor_scalar(nodeI[:, :], work, float(ZERO), None, ALU.add))
                dve.wait_ge(plan_hf, 1)
                for b, r in BLOCKS:
                    def o(k):
                        return op[0:r, b, k:k + 1]
                    link(dve.scalar_tensor_tensor(work[0:r], iota[0:r, 0:NT], o(HI), psS[b][0:r, 0:NT],
                                                  ALU.is_equal, ALU.mult))
                    link(dve.tensor_reduce(o(HEAD), work[0:r], AX.X, ALU.add))
                    link(dve.tensor_tensor(o(BEGUN), o(HEAD), o(START), ALU.is_lt))
                    link(dve.tensor_scalar(o(PREV), o(START), float(-P), None, ALU.add))
                    link(dve.scalar_tensor_tensor(o(NEXT), o(HEAD), o(PREV), o(BEGUN), ALU.is_ge, ALU.mult))
                    link(copy(ixf[0:r, b:b + 1], o(HEAD)))
                    link(dve.scalar_tensor_tensor(o(NEXT), o(HEAD), float(-FAR), o(NEXT), ALU.add, ALU.mult))
                    link(dve.tensor_scalar(ixf[0:r, 2 + b:3 + b], o(NEXT), float(FAR), None, ALU.add))
                    link(dve.tensor_scalar(mendM[0:r, b, :], psM[0:r, 2 * P:2 * P + ET], o(DST), o(BEGUN),
                                           ALU.is_equal, ALU.mult))
                dve.sem_inc(plan_done, 1)

            def take_z(i, c, l):
                t, s, n = at(i, c, 2)
                dve.wait_ge(z_ps[s], l * uses(s) + n + 1)
                dve.tensor_tensor(kept(t), psY[s][:, :], bvec[:, :], ALU.add).then_inc(z_sb[s], 1)

            def select(i, c, l):
                t, g, n = at(i, c, 4)
                dve.wait_ge(seg_ps[g], l * uses(g) + n)
                dve.tensor_scalar(sel[:, g, :], iota[:, :], col(headT, t), None, ALU.is_equal)\
                   .then_inc(sel_set[g], 1)

            def low(i, c, l):
                t, g, n = at(i, c, 4)
                dve.wait_ge(hi_set[g], l * uses(g) + n + 1)
                dve.tensor_tensor(parts[:, g % 2, 1, :], rows[:, g, :], parts[:, g % 2, 0, :].bitcast(F32),
                                  ALU.subtract).then_inc(lo_set[g], 1)

            def sage(i, c, k, rows_out, out_op, one):
                t, s, n = at(i, c, 2)
                dve.wait_ge(node_in[s], 16 * ((k - 1) * uses(s) + n + 1))
                dve.wait_ge(xT_ps[s], k * uses(s) + n)
                a, v = rows[:, s, :], rows[:, 2 + s, :]
                one(dve.scalar_tensor_tensor(a, a, col(rdeg, t), kept(t), ALU.mult, ALU.add))
                one(dve.scalar_tensor_tensor(v, a, 0.0, avec[:, :], ALU.min, ALU.mult))
                out_op(dve.scalar_tensor_tensor(rows_out, a, 0.0, v, ALU.max, ALU.add))

            def next_x(i, c, k):
                t, s, n = at(i, c, 2)
                sage(i, c, k, rows[:, 2 + s, :], lambda ins: ins.then_inc(xn_ready[s], 1), linker(t, 2))

            for l in range(LAYERS):
                if l == 0:
                    make_plan()
                dve.wait_ge(bvec_in, 16 * (l + 1))
                for e in range(2):
                    select(0, e, l)
                    low(0, e, l)
                for i in turns(dve, PAIRS - 1, l == 0):
                    for c in range(2):
                        take_z(i, c, l)
                        for e in (2 * c + 2, 2 * c + 3):
                            select(i, e, l)
                            low(i, e, l)
                take_z(PAIRS - 1, 0, l)
                for e in (2, 3):
                    select(PAIRS - 1, e, l)
                    low(PAIRS - 1, e, l)
                take_z(PAIRS - 1, 1, l)
                select(PAIRS, 0, l)
                low(PAIRS, 0, l)
                take_z(PAIRS, 0, l)
                dve.wait_ge(mend_g, 32 * (l + 1))
                for b, r in BLOCKS:
                    dve.wait_ge(mend_ps, 2 * l + b + 1)
                    dve.tensor_tensor(rows[0:r, 2 + b, :], rows[0:r, 2 + b, :], psS[b][0:r, :], ALU.add)\
                       .then_inc(mend_add, 1)
                dve.wait_ge(avec_in, 16 * (l + 1))
                all_turns(dve, z_sb, l + 1)
                if l + 1 < LAYERS:
                    each_pair(dve, lambda i, c: next_x(i, c, l + 1), False)
                    done[0] += 2 * NT

            def residual(i, c, one):
                t, s, n = at(i, c, 2)
                a = rows[:, s, :]
                dve.wait_ge(xe_in[s], 16 * (n + 1))
                sage(i, c, LAYERS, a, one, one)
                one(dve.tensor_tensor(kept(t), a, outs[:, s, :], ALU.add))
                moments(s, kept(t), one)

            def norm_end(i, c):
                t, s, n = at(i, c, 2)
                normed(i, c, 1, kept(t))

            def logits(i, c, one):
                t, s, n = at(i, c, 2)
                dve.wait_ge(lg_ps[s], n + 1)
                one(dve.tensor_tensor(sm[:, s, LG:LG + X], psM[:, 0:X], bgs[:, :], ALU.add))
                one(dve.tensor_reduce(st[:, s, 9:10], sm[:, s, LG:LG + X], AX.X, ALU.max))
                dve.tensor_scalar(st[:, s, 9:10], st[:, s, 9:10], -1.0, None, ALU.mult).then_inc(lg_sb[s], 1)

            def weights(i, c, one):
                t, s, n = at(i, c, 2)
                dve.wait_ge(p_sb[s], n + 1)
                dve.wait_ge(cw_ps[s], n)
                p, top = sm[:, s, PR:PR + X], sm[:, s, TOP:TOP + X]
                one(dve.reciprocal(st[:, s, 11:12], st[:, s, 10:11]))
                one(dve.tensor_scalar(p, p, st[:, s, 11:12], None, ALU.mult))
                carry()
                one(dve.max(top, p))
                carry()
                one(dve.max_index(smi[:, :], top, p))
                one(dve.tensor_copy(st[:, s, 9:11], smi[:, 0:2]))
                one(dve.tensor_scalar(sm[:, s, LG:LG + X], iota[:, 0:X], st[:, s, 10:11],
                                      top[:, 1:2], ALU.is_equal, ALU.mult))
                one(dve.tensor_scalar(p, iota[:, 0:X], st[:, s, 9:10], top[:, 0:1], ALU.is_equal, ALU.mult))
                dve.tensor_tensor(sm[:, s, CW:CW + X], p, sm[:, s, LG:LG + X], ALU.add).then_inc(cw_set[s], 1)
                dve.wait_ge(cw_set[s], n + 1)

            def hidden(i, c, one):
                t, s, n = at(i, c, 2)
                h = outs[:, 2 + s, :]
                h3 = h.rearrange("p (e f) -> p e f", e=X)
                dve.wait_ge(y_ps[s], LAYERS * uses(s) + n + 1)
                dve.wait_ge(hT_ps[s], n)
                one(dve.tensor_tensor(h, psY[s][:, :], bvec[:, :], ALU.add))
                dve.scalar_tensor_tensor(h3, h3, 0.0, sm[:, s, CW:CW + X].unsqueeze(2).to_broadcast([P, X, F]),
                                         ALU.max, ALU.mult).then_inc(hg_sb[s], 1)

            def finish(i, c):
                t, s, n = at(i, c, 2)
                dve.wait_ge(o_ps[s], n + 1)
                dve.tensor_tensor(kept(t), psH[:, :], kept(t), ALU.add).then_inc(o_sb[s], 1)

            dve.wait_ge(bvec_in, 16 * (LAYERS + 1))
            dve.wait_ge(small_in, 48)
            residual(0, 0, link)
            norm_end(0, 0)
            residual(0, 1, link)
            norm_end(0, 1)
            logits(0, 0, link)
            residual(0, 2, link)
            weights(0, 0, link)
            norm_end(0, 2)
            hidden(0, 0, link)
            LINKS = 2 + 6 + 7 + 1
            for i in turns(dve, PAIRS - 1, True):
                for c in (1, 2):
                    one = linker(2 * i + (c - 1), LINKS)
                    logits(i, c, one)
                    residual(i, c + 2, one)
                    weights(i, c, one)
                    norm_end(i, c + 2)
                    hidden(i, c, one)
                    finish(i, c - 1)
            done[0] += LINKS * 2 * (PAIRS - 1)
            for i, c in ((PAIRS - 1, 1), (PAIRS, 0)):
                logits(i, c, link)
                weights(i, c, link)
                hidden(i, c, link)
                finish(i, c - 1)
            finish(PAIRS, 0)


_INS = ["x", "src", "dst"] + [f"L0_gnn_{k}{l}" for l in range(3) for k in ("Wl", "bl", "Wr", "a")] \
    + [f"L0_ffn_{k}" for k in ("Wr", "br", "W1", "b1", "W2", "b2")]


def kernel(**inputs):
    import numpy as _np
    import concourse.bacc as _bacc
    from concourse import mybir as _mybir
    from concourse.bass_utils import run_bass_kernel_spmd as _run

    nc = _bacc.Bacc("TRN2", target_bir_lowering=False, num_devices=1)
    arrays, aps = {}, {}
    for name in _INS:
        a = _np.ascontiguousarray(inputs[name])
        arrays[f"in_{name}"] = a
        aps[name] = nc.dram_tensor(f"in_{name}", a.shape, _mybir.dt.from_np(a.dtype), kind="ExternalInput").ap()
    out = nc.dram_tensor("out_rows", inputs["x"].shape, F32, kind="ExternalOutput").ap()
    gnn = {k: [aps[f"L0_gnn_{k}{l}"] for l in range(3)] for k in ("Wl", "bl", "Wr", "a")}
    build(nc, aps["x"], aps["src"], aps["dst"], gnn["Wl"], gnn["bl"], gnn["Wr"], gnn["a"],
          *(aps[f"L0_ffn_{k}"] for k in ("Wr", "br", "W1", "b1", "W2", "b2")), out)
    r = _run(nc, [arrays], core_ids=[0])
    return r.results[0]["out_rows"]
```

```python
from contextlib import ExitStack

import concourse.bass as bass
from concourse import mybir

ALU = mybir.AluOpType
ACT = mybir.ActivationFunctionType
AX = mybir.AxisListType
F32 = mybir.dt.float32
F32R = mybir.dt.float32r
BF16 = mybir.dt.bfloat16
I32 = mybir.dt.int32
U32 = mybir.dt.uint32

P = 128
EPS = 1e-5
FAR = 1 << 22


def at(i, c, ring):
    return i * ring + c, c % ring, i + c // ring


def build(nc, x, src, dst, Wl, bl, Wr, al, Wg, bg, W1, b1, W2, b2, out):
    N, D = x.shape
    E = src.shape[0]
    X = W1.shape[0]
    F = W1.shape[2]
    C = D // P
    LAYERS = len(Wl)
    NT = -(-N // P)
    ET = -(-E // P)
    ER = E - (ET - 1) * P
    NR = N - (NT - 1) * P
    PAIRS = NT // 2
    assert D == 512 and X * F == 512 and X == 8 and NT == 2 * PAIRS + 1 and ET == 4 * PAIRS + 1
    EB = ET - P
    ZERO = ET * P
    BLOCKS = [(0, P), (1, EB)]

    def uses(slot):
        return PAIRS + (slot == 0)

    y_d = nc.dram_tensor("y_rows", (NT * P, D), F32, kind="Internal").ap()
    s_d = nc.dram_tensor("sum_rows", (ET * P + 1, D), F32, kind="Internal").ap()

    with ExitStack() as ctx:
        def sb(name, shape, dt=F32):
            return ctx.enter_context(nc.sbuf_tensor(name, shape, dt))

        def pb(name, shape, dt=F32):
            return ctx.enter_context(nc.psum_tensor(name, shape, dt))

        def sem(name):
            return ctx.enter_context(nc.semaphore(name))

        def sems(name, n):
            return [sem(f"{name}{k}") for k in range(n)]

        res = sb("res", [P, NT, D])
        wy_at = nc.sbuf_base
        wy = sb("wy", [P, C, D])
        wz = sb("wz", [P, C, D])
        rows = sb("rows", [P, 4, D])
        outs = sb("outs", [P, 4, D])
        xTs = sb("xTs", [P, 2, C, P])
        hTs_at = nc.sbuf_base
        hTs = sb("hTs", [P, 2, C, P])
        bvec = sb("bvec", [P, D])
        avec = sb("avec", [P, D])
        b2s = sb("b2s", [4 * X, D], F32R)
        ident = sb("ident", [P, P])
        iota = sb("iota", [P, P])
        lists_at = nc.sbuf_base
        lists = sb("lists", [P, 2 * ET])
        nodeI = sb("nodeI", [P, NT], I32)
        rdeg = sb("rdeg", [P, NT])
        small = sb("small", [P, 15])
        ixe, ixn, ixf = (small[:, k:k + n].bitcast(I32) for k, n in ((0, 4), (4, 2), (6, 4)))
        half, scrap = small[:, 10:11], small[0:1, 11:15]
        wgs = sb("wgs", [P, C, X])
        bgs = sb("bgs", [P, X])
        st = sb("st", [P, 2, 17])
        sm = sb("sm", [P, 2, 8 * X])
        LG, EX, TOP, CW, HIGH, LOW = (X * k for k in (0, 1, 2, 3, 4, 6))
        STAT, MEAN, VAR, RSTD, SHIFT, LOWEST, SUM, INV, IDX, TOPW = 0, 6, 7, 8, 9, 10, 11, 12, 13, 15
        op = sb("op", [P, 2, 8])
        LO, HI, DST, START, HEAD, BEGUN, NEXT, PREV = range(8)

        hTs0 = hTs[:, 0].rearrange("p c n -> p (c n)")
        hTs1 = hTs[:, 1].rearrange("p c n -> p (c n)")
        srcT = lists[:, 0:ET].bitcast(I32)
        headT = lists[:, ET:2 * ET]
        cwT = nc.alloc_sbuf_tensor_at("cwT", [4 * X, 2, P], F32R, offset=lists_at)
        parts = nc.alloc_sbuf_tensor_at("parts", [P, 2, 2, D], F32R, offset=wy_at)
        sel = nc.alloc_sbuf_tensor_at("sel", [P, 4, P], F32R, offset=hTs_at)
        lower, ones, first = (hTs[:, 0, k, :] for k in range(3))
        onehot = hTs1.bitcast(BF16).rearrange("p (g n) -> p g n", g=4)
        mendM = hTs1[:, 0:2 * ET].rearrange("p (b t) -> p b t", b=2)
        openlo = [hTs1[:, 320:320 + P], outs[:, 3, 320:320 + P]]
        loT = outs[:, 3, 0:ET]
        hiT = outs[:, 3, ET:2 * ET]
        counts, colsum, starts, work = (outs[:, 2, 80 * k:80 * k + NT] for k in range(4))
        dstT = outs[:, 2, 320:320 + ET]

        def tmp(k, n=P):
            return res[:, NT - 8 + k // 4, (k % 4) * P:(k % 4) * P + n]

        ints = {"src": (0, 1), "dst": (2, 3), "lo": (4, 5), "hi": (6, 7)}
        flts = {"src": (8, 9), "lo": (10, 11), "hi": (12, 13), "head": (14, 15), "dst": (16, 17), "val": (18, 19)}
        smi = lists[:, 2 * P:2 * P + 8].bitcast(U32)
        zeros = tmp(24, D)
        b2raw = tmp(20, D)[0:4 * X]
        b2high = tmp(28, D)[0:4 * X]
        group = outs[0:4 * X, 0, 0:1].bitcast(I32)
        is_low, is_high = outs[0:4 * X, 0, 1:2], outs[0:4 * X, 0, 2:3]

        def int_rows(name, b):
            return tmp(ints[name][b]).bitcast(I32)

        def flt_rows(name, b):
            return tmp(flts[name][b])

        psT = [pb(f"psT{s}", [P, D]) for s in range(2)]
        psY = [pb(f"psY{s}", [P, D]) for s in range(2)]
        psS = [pb(f"psS{s}", [P, D]) for s in range(2)]
        psH = pb("psH", [P, D])
        psM = pb("psM", [P, D])

        ids_pad = sem("ids_pad")
        ids_in = sem("ids_in")
        const_set = sem("const_set")
        small_in = sem("small_in")
        b2_in = sem("b2_in")
        b2_set = sem("b2_set")
        zero_set = sem("zero_set")
        zero_st = sem("zero_st")
        rows_set = sem("rows_set")
        lists_ps = sem("lists_ps")
        lists_set = sem("lists_set")
        plan_in = sem("plan_in")
        plan_ps = sem("plan_ps")
        plan_rp = sem("plan_rp")
        plan_hf = sem("plan_hf")
        plan_done = sem("plan_done")
        wy_in = sem("wy_in")
        wz_in = sem("wz_in")
        bvec_in = sem("bvec_in")
        avec_in = sem("avec_in")
        x_in = sems("x_in", 2)
        xe_in = sems("xe_in", 2)
        ix_n = sems("ix_n", 2)
        node_in = sems("node_in", 2)
        vchain = sem("vchain")
        xn_ready = sems("xn_ready", 2)
        xT_ps = sems("xT_ps", 2)
        xT_sb = sems("xT_sb", 2)
        xT_kept = sems("xT_kept", 2)
        y_ps = sems("y_ps", 2)
        y_sb = sems("y_sb", 2)
        y_st = sems("y_st", 2)
        var_in = sems("var_in", 2)
        rstd_in = sems("rstd_in", 2)
        shift_in = sems("shift_in", 2)
        oh_set = sems("oh_set", 4)
        oh_used = sems("oh_used", 4)
        ix_e = sems("ix_e", 4)
        edge_in = sems("edge_in", 4)
        hi_set = sems("hi_set", 4)
        lo_set = sems("lo_set", 4)
        sel_set = sems("sel_set", 4)
        seg_ps = sems("seg_ps", 4)
        seg_sb = sems("seg_sb", 4)
        seg_st = sems("seg_st", 4)
        xT_back = sems("xT_back", 2)
        z_ps = sems("z_ps", 2)
        z_sb = sems("z_sb", 2)
        mend_in = sem("mend_in")
        mend_g = sem("mend_g")
        mend_ps = sem("mend_ps")
        mend_add = sem("mend_add")
        mend_st = sem("mend_st")
        lg_ps = sems("lg_ps", 2)
        lg_sb = sems("lg_sb", 2)
        p_sb = sems("p_sb", 2)
        cw_set = sems("cw_set", 2)
        hg_sb = sems("hg_sb", 2)
        cw_ps = sems("cw_ps", 2)
        cw_sb = sems("cw_sb", 2)
        hT_ps = sems("hT_ps", 2)
        hT_sb = sems("hT_sb", 2)
        o_ps = sems("o_ps", 2)
        o_sb = sems("o_sb", 2)
        o_st = sems("o_st", 2)

        block = ctx.enter_context(nc.Block())

        def all_turns(eng, signals, rounds, step=1):
            for slot, s in enumerate(signals):
                eng.wait_ge(s, rounds * uses(slot) * step)

        def turns(eng, n, fresh):
            if fresh:
                yield 0
            with eng.Fori(1 if fresh else 0, n) as i:
                yield i

        def each_pair(eng, step, fresh):
            for i in turns(eng, PAIRS, fresh):
                for c in range(2):
                    step(i, c)
            step(PAIRS, 0)

        def each_four(eng, step, fresh):
            for i in turns(eng, PAIRS, fresh):
                for c in range(4):
                    step(i, c)
            step(PAIRS, 0)

        def rows_of(t, n=P):
            return slice(t * P, t * P + n) if isinstance(t, int) else bass.ds(t * P, n)

        def kept(t, n=P):
            return res[0:n, t, :] if isinstance(t, int) else res[0:n, bass.ds(t, 1), :].rearrange("p a d -> p (a d)")

        def col(table, t):
            return table[:, t:t + 1] if isinstance(t, int) else table[:, bass.ds(t, 1)]

        def load_x(eng, i, c, ring, read, rounds, signal):
            t, s, n = at(i, c, 2)
            eng.wait_ge(read[s], rounds * uses(s) + n)
            r = NR if isinstance(t, int) and t == NT - 1 else P
            eng.dma_start(ring[0:r, s, :], x[rows_of(t, r)]).then_inc(signal[s], 16)

        @block.sync
        def _(sp):
            def load_w(buf, w, signal):
                sp.dma_start(buf[:, :, :], w.rearrange("(c p) n -> p c n", p=P)).then_inc(signal, 16)

            def load_row(buf, v, signal):
                sp.dma_start(buf[:, :], v.partition_broadcast(P)).then_inc(signal, 16)

            def store_y(i, c, k):
                t, s, n = at(i, c, 2)
                sp.wait_ge(y_sb[s], k * uses(s) + n + 1)
                sp.dma_start(y_d[rows_of(t)], outs[:, s, :]).then_inc(y_st[s], 16)

            sp.wait_ge(ids_pad, 2)
            for name, v in (("src", src), ("dst", dst)):
                sp.dma_start(int_rows(name, 0), v[0:P * P].rearrange("(t p) -> t p", p=P)).then_inc(ids_in, 16)
                sp.dma_start(int_rows(name, 1)[0:EB - 1], v[P * P:E - ER].rearrange("(t p) -> t p", p=P))\
                  .then_inc(ids_in, 16)
                sp.dma_start(int_rows(name, 1)[EB - 1:EB, 0:ER], v[E - ER:E].rearrange("(t p) -> t p", p=ER))\
                  .then_inc(ids_in, 16)
            load_w(wy, Wl[0], wy_in)
            for k in range(4):
                sp.dma_start(b2raw[k * X:(k + 1) * X, :], b2).then_inc(b2_in, 16)
            sp.wait_ge(zero_set, 1)
            sp.dma_start(s_d[ZERO:ZERO + 1], zeros[0:1, :]).then_inc(zero_st, 16)
            load_w(wz, Wr[0], wz_in)
            load_row(bvec, bl[0], bvec_in)
            load_row(avec, al[0], avec_in)
            load_row(bgs, bg, small_in)
            sp.dma_start(wgs[:, :, :], Wg.rearrange("(c p) n -> p c n", p=P)).then_inc(small_in, 16)
            each_pair(sp, lambda i, c: store_y(i, c, 0), True)

            def store_seg(i, c, l):
                t, g, n = at(i, c, 4)
                sp.wait_ge(seg_sb[g], l * uses(g) + n + 1)
                sp.dma_start(s_d[rows_of(t)], outs[:, g, :]).then_inc(seg_st[g], 16)

            for l in range(LAYERS):
                if l > 0:
                    all_turns(sp, xn_ready, l + 1)
                    load_row(avec, al[l], avec_in)
                each_four(sp, lambda i, c: store_seg(i, c, l), l == 0)
                for g in range(4):
                    sp.wait_ge(seg_ps[g], (l + 1) * uses(g))
                if l + 1 < LAYERS:
                    load_w(wy, Wl[l + 1], wy_in)
                else:
                    for e in range(X):
                        sp.dma_start(wy[:, :, e * F:(e + 1) * F], W1[e].rearrange("(c p) f -> p c f", p=P))\
                          .then_inc(wy_in, 16)
                for g in range(4):
                    sp.wait_ge(seg_st[g], 16 * (l + 1) * uses(g))
                starts_d = s_d[0:ET * P].rearrange("(t p) d -> t p d", p=P)[:, 0, :]
                for b, r in BLOCKS:
                    sp.dma_start(rows[0:r, b, :], starts_d[b * P:b * P + r]).then_inc(mend_in, 16)
                all_turns(sp, z_sb, l + 1)
                if l + 1 < LAYERS:
                    load_w(wz, Wr[l + 1], wz_in)
                    load_row(bvec, bl[l + 1], bvec_in)
                    each_pair(sp, lambda i, c: store_y(i, c, l + 1), False)
                else:
                    load_w(wz, W2.rearrange("e f d -> (e f) d"), wz_in)
                    load_row(bvec, b1.rearrange("e f -> (e f)"), bvec_in)

            def store_out(i, c, r=P):
                t, s, n = at(i, c, 2)
                sp.wait_ge(o_sb[s], n + 1)
                sp.dma_start(out[rows_of(t, r)], kept(t, r)).then_inc(o_st[s], 16)

            for c in range(4):
                load_x(sp, 0, c, outs, var_in, 1, xe_in)
            for i in turns(sp, PAIRS - 2, True):
                for c in range(2):
                    load_x(sp, i, c + 4, outs, var_in, 1, xe_in)
                    store_out(i, c)
            load_x(sp, PAIRS, 0, outs, var_in, 1, xe_in)
            for c in range(4):
                store_out(PAIRS - 2, c)
            store_out(PAIRS, 0, NR)
            all_turns(sp, o_st, 1, 16)
            sp.wait_ge(zero_st, 16)

        @block.gpsimd
        def _(pool):
            pool.memset(int_rows("src", 1), 0).then_inc(ids_pad, 1)
            pool.memset(int_rows("dst", 1), -1).then_inc(ids_pad, 1)
            pool.iota(iota[:, :], pattern=[[1, P]], base=0, channel_multiplier=0,
                      allow_small_or_imprecise_dtypes=True).then_inc(const_set, 1)
            pool.memset(ident[:, :], 0.0).then_inc(const_set, 1)
            pool.memset(hTs0[:, 0:2 * P], 1.0).then_inc(const_set, 1)
            pool.memset(hTs0[:, 2 * P:3 * P], 0.0).then_inc(const_set, 1)
            pool.memset(zeros[0:1, :], 0.0).then_inc(zero_set, 1)
            pool.wait_ge(const_set, 4)
            pool.affine_select(out=ident[:, :], in_=ident[:, :], compare_op=ALU.not_equal, fill=1.0, base=0,
                               pattern=[[-1, P]], channel_multiplier=1).then_inc(const_set, 1)
            pool.affine_select(out=lower, in_=lower, compare_op=ALU.is_gt, fill=0.0, base=0,
                               pattern=[[1, P]], channel_multiplier=-1).then_inc(const_set, 1)
            pool.memset(first[0:1, :], 1.0).then_inc(const_set, 1)
            for b, r in BLOCKS:
                pool.iota(op[:, b, START:START + 1], pattern=[[0, 1]], base=b * P * P, channel_multiplier=P,
                          allow_small_or_imprecise_dtypes=True).then_inc(const_set, 1)

            pool.iota(group, pattern=[[0, 1]], base=0, channel_multiplier=1).then_inc(const_set, 1)
            pool.memset(half, -0.5).then_inc(const_set, 1)
            pool.wait_ge(const_set, 11)

            def rstd(i, c, k):
                t, s, n = at(i, c, 2)
                pool.wait_ge(var_in[s], k * uses(s) + n + 1)
                pool.tensor_tensor(st[:, s, RSTD:RSTD + 1], st[:, s, VAR:VAR + 1], half, ALU.pow)\
                    .then_inc(rstd_in[s], 1)

            load_x(pool, 0, 0, rows, xn_ready, 0, x_in)
            load_x(pool, 0, 1, rows, xn_ready, 0, x_in)
            for i in turns(pool, PAIRS - 1, True):
                for c in range(2):
                    rstd(i, c, 0)
                    load_x(pool, i, c + 2, rows, xn_ready, 0, x_in)
            rstd(PAIRS - 1, 0, 0)
            load_x(pool, PAIRS, 0, rows, xn_ready, 0, x_in)
            rstd(PAIRS - 1, 1, 0)
            rstd(PAIRS, 0, 0)

            def gather_edge(i, c, l):
                t, g, n = at(i, c, 4)
                used = l * uses(g) + n
                pool.wait_ge(lo_set[g], used)
                pool.tensor_copy(ixe[:, g:g + 1], col(srcT, t)).then_inc(ix_e[g], 1)
                pool.wait_ge(ix_e[g], used + 1)
                pool.indirect_dma_start(out=rows[:, g, :], out_offset=None, in_=y_d,
                                        in_offset=bass.IndirectOffsetOnAxis(ap=ixe[:, g:g + 1], axis=0),
                                        bounds_check=i + (NT * P - 1 + c)).then_inc(edge_in[g], 16)

            def gather_node(i, c, l, read=xn_ready):
                t, s, n = at(i, c, 2)
                used = l * uses(s) + n
                pool.wait_ge(read[s], (uses(s) if read is var_in else (l + 1) * uses(s)) + n)
                pool.tensor_copy(ixn[:, s:s + 1], col(nodeI, t)).then_inc(ix_n[s], 1)
                pool.wait_ge(ix_n[s], used + 1)
                pool.indirect_dma_start(out=rows[:, s, :], out_offset=None, in_=s_d,
                                        in_offset=bass.IndirectOffsetOnAxis(ap=ixn[:, s:s + 1], axis=0),
                                        bounds_check=i + (ZERO + c)).then_inc(node_in[s], 16)

            for l in range(LAYERS):
                if l == 0:
                    pool.wait_ge(lists_set, 1)
                all_turns(pool, y_st, l + 1, 16)
                each_four(pool, lambda i, c: gather_edge(i, c, l), l == 0)
                for g in range(4):
                    pool.wait_ge(seg_st[g], 16 * (l + 1) * uses(g))
                if l == 0:
                    pool.wait_ge(plan_done, 1)
                    pool.wait_ge(zero_st, 16)
                for b, r in BLOCKS:
                    pool.indirect_dma_start(out=rows[0:r, 2 + b, :], out_offset=None, in_=s_d,
                                            in_offset=bass.IndirectOffsetOnAxis(ap=ixf[0:r, b:b + 1], axis=0),
                                            bounds_check=ZERO).then_inc(mend_g, 16)
                pool.wait_ge(mend_in, 32 * (l + 1))
                pool.wait_ge(mend_g, 32 * (l + 1))
                for b, r in BLOCKS:
                    pool.wait_ge(mend_add, 2 * l + b + 1)
                    pool.indirect_dma_start(out=s_d, out_offset=bass.IndirectOffsetOnAxis(
                                                ap=ixf[0:r, 2 + b:3 + b], axis=0),
                                            in_=rows[0:r, 2 + b, :], in_offset=None,
                                            bounds_check=ZERO, oob_is_err=False).then_inc(mend_st, 16)
                pool.wait_ge(mend_st, 32 * (l + 1))
                if l + 1 < LAYERS:
                    each_pair(pool, lambda i, c: gather_node(i, c, l), l == 0)
            gather_node(0, 0, LAYERS - 1)
            gather_node(0, 1, LAYERS - 1)
            def scale_shift(i, c):
                t, s, n = at(i, c, 2)
                rstd(i, c, 1)
                pool.wait_ge(rstd_in[s], uses(s) + n + 1)
                pool.tensor_tensor(st[:, s, SHIFT:SHIFT + 1], st[:, s, MEAN:MEAN + 1], st[:, s, RSTD:RSTD + 1],
                                   ALU.mult).then_inc(shift_in[s], 1)

            for i in turns(pool, PAIRS - 1, True):
                for c in range(2):
                    scale_shift(i, c)
                    gather_node(i, c + 2, LAYERS - 1, var_in)
            scale_shift(PAIRS - 1, 0)
            gather_node(PAIRS, 0, LAYERS - 1, var_in)
            scale_shift(PAIRS - 1, 1)
            scale_shift(PAIRS, 0)

        @block.tensor
        def _(pe):
            def transposes(dest, tile, signal=None):
                for c in range(C):
                    mm = pe.transpose(dest[:, c * P:(c + 1) * P], tile[:, c * P:(c + 1) * P], ident[:, :])
                if signal is not None:
                    mm.then_inc(signal, 1)

            def product(dest, xT, w, signal=None, last=True):
                for c in range(C):
                    mm = pe.matmul(dest, xT[:, c, :], w[:, c, :], start=(c == 0), stop=(last and c == C - 1))
                if signal is not None:
                    mm.then_inc(signal, 1)

            pe.wait_ge(const_set, 10)
            pe.wait_ge(rows_set, 1)
            for b, r in BLOCKS:
                for k, name in enumerate(("src", "lo", "hi", "head")):
                    mm = pe.transpose(psS[b][:, k * P:k * P + r], flt_rows(name, b)[0:r, :], ident[0:r, 0:r])
                mm.then_inc(lists_ps, 1)

            def x_transpose(i, c, k):
                t, s, n = at(i, c, 2)
                pe.wait_ge(xn_ready[s], k * uses(s) + n + 1)
                pe.wait_ge(xT_kept[s], k * uses(s) + n)
                transposes(psT[s], rows[:, 2 + s, :], xT_ps[s])

            def y_product(i, c, k):
                t, s, n = at(i, c, 2)
                pe.wait_ge(xT_sb[s], k * uses(s) + n + 1)
                pe.wait_ge(y_sb[s], k * uses(s) + n)
                product(psY[s][:, :], xTs[:, s], wy, y_ps[s])

            def count(i, c, start=False):
                t, g, n = at(i, c, 4)
                pe.wait_ge(oh_set[g], 2 * (n + 1))
                pe.matmul(psH[:, 0:NT], onehot[:, g, 0:P], onehot[:, g, P:P + NT], start=start, stop=True,
                          skip_group_check=True).then_inc(oh_used[g], 1)

            def dense(k):
                pe.wait_ge(wy_in, 16 * (k + 1))
                if k > 0:
                    all_turns(pe, z_sb, k)
                x_transpose(0, 0, k)
                if k == 0:
                    count(0, 0, True)
                for i in turns(pe, PAIRS, k == 0):
                    for c in range(2):
                        x_transpose(i, c + 1, k)
                        y_product(i, c, k)
                        if k == 0:
                            count(i, 2 * c + 1)
                            count(i, 2 * c + 2)
                y_product(PAIRS, 0, k)

            def make_plan():
                pe.wait_ge(plan_in, 1)
                pe.matmul(psM[:, 0:NT], lower, counts, start=True, stop=True)
                pe.matmul(psM[:, P:P + NT], ones, counts, start=True, stop=True)
                pe.matmul(psM[:, 2 * P:2 * P + ET], first, dstT, start=True, stop=True)
                for b, r in BLOCKS:
                    mm = pe.transpose(psH[:, (1 + b) * P:(1 + b) * P + r], openlo[b][0:r, :], ident[0:r, 0:r])
                mm.then_inc(plan_ps, 1)
                pe.wait_ge(plan_rp, 1)
                for b, r in BLOCKS:
                    mm = pe.matmul(psS[b][0:r, 0:NT], openlo[b][:, 0:r], starts, start=True, stop=True)
                mm.then_inc(plan_hf, 1)

            def z_product(i, c, l):
                t, s, n = at(i, c, 2)
                pe.wait_ge(xT_back[s], l * uses(s) + n + 1)
                pe.wait_ge(z_sb[s], l * uses(s) + n)
                product(psY[s][:, :], xTs[:, s], wz, z_ps[s])

            def segment_sum(i, c, l):
                t, g, n = at(i, c, 4)
                used = l * uses(g) + n
                before = (g + 2) % 4
                pe.wait_ge(seg_sb[before], l * uses(before) + n + (g >= 2))
                pe.wait_ge(sel_set[g], used + 1)
                pe.wait_ge(hi_set[g], used + 1)
                pe.wait_ge(lo_set[g], used + 1)
                pe.matmul(psS[g % 2][:, :], sel[:, g, :], parts[:, g % 2, 0, :], start=True, stop=False)
                pe.matmul(psS[g % 2][:, :], sel[:, g, :], parts[:, g % 2, 1, :], start=False, stop=True)\
                  .then_inc(seg_ps[g], 1)

            for l in range(LAYERS):
                dense(l)
                if l == 0:
                    make_plan()
                all_turns(pe, y_sb, l + 1)
                pe.wait_ge(wz_in, 16 * (l + 1))
                for i in turns(pe, PAIRS, l == 0):
                    for c in range(2):
                        z_product(i, c, l)
                        segment_sum(i, 2 * c, l)
                        segment_sum(i, 2 * c + 1, l)
                z_product(PAIRS, 0, l)
                segment_sum(PAIRS, 0, l)
                for g in range(4):
                    pe.wait_ge(seg_sb[g], (l + 1) * uses(g))
                pe.wait_ge(mend_in, 32 * (l + 1))
                for b, r in BLOCKS:
                    for kb, kr in BLOCKS:
                        mm = pe.matmul(psS[b][0:r, :], mendM[0:kr, kb, b * P:b * P + r], rows[0:kr, kb, :],
                                       start=(kb == 0), stop=(kb == 1))
                    mm.then_inc(mend_ps, 1)

            def x_turn(i, c):
                t, s, n = at(i, c, 2)
                pe.wait_ge(xn_ready[s], LAYERS * uses(s) + n + 1)
                pe.wait_ge(xT_sb[s], LAYERS * uses(s) + n)
                transposes(psT[s], rows[:, 2 + s, :], xT_ps[s])

            def router(i, c, first=False):
                t, s, n = at(i, c, 2)
                pe.wait_ge(xT_sb[s], LAYERS * uses(s) + n + 1)
                _, so, no = at(i, c - 1, 2)
                if not first:
                    pe.wait_ge(lg_sb[so], no + 1)
                product(psM[:, 0:X], xTs[:, s], wgs, lg_ps[s])

            def up(i, c):
                t, s, n = at(i, c, 2)
                pe.wait_ge(hg_sb[s], n)
                product(psY[s][:, :], xTs[:, s], wy, y_ps[s])

            def hidden_turn(i, c, first=False):
                t, s, n = at(i, c, 2)
                _, so, no = at(i, c - 1, 2)
                pe.wait_ge(hg_sb[s], n + 1)
                if not first:
                    pe.wait_ge(hT_sb[so], no + 1)
                    pe.wait_ge(cw_sb[so], no + 1)
                transposes(psS[0], outs[:, 2 + s, :], hT_ps[s])
                pe.wait_ge(cw_set[s], n + 1)
                pe.transpose(psS[1][0:4 * X, 0:P], sm[:, s, HIGH:HIGH + 4 * X], ident[:, :])\
                  .then_inc(cw_ps[s], 1)

            def down(i, c, first=False):
                t, s, n = at(i, c, 2)
                _, so, no = at(i, c - 1, 2)
                if not first:
                    pe.wait_ge(o_sb[so], no + 1)
                pe.wait_ge(hT_sb[s], n + 1)
                product(psH[:, :], hTs[:, s], wz, last=False)
                pe.wait_ge(cw_sb[s], n + 1)
                pe.matmul(psH[:, :], cwT[:, s, :], b2s[:, :], start=False, stop=True).then_inc(o_ps[s], 1)

            pe.wait_ge(wy_in, 16 * (LAYERS + X))
            pe.wait_ge(wz_in, 16 * (LAYERS + 1))
            pe.wait_ge(small_in, 32)
            pe.wait_ge(b2_set, 1)
            x_turn(0, 0)
            x_turn(0, 1)
            router(0, 0, True)
            up(0, 0)
            for i in turns(pe, PAIRS - 1, True):
                for c in (1, 2):
                    start = isinstance(i, int) and c == 1
                    x_turn(i, c + 1)
                    router(i, c)
                    hidden_turn(i, c - 1, start)
                    up(i, c)
                    down(i, c - 1, start)
            x_turn(PAIRS - 1, 2)
            for c in (1, 2):
                router(PAIRS - 1, c)
                hidden_turn(PAIRS - 1, c - 1)
                up(PAIRS - 1, c)
                down(PAIRS - 1, c - 1)
            hidden_turn(PAIRS, 0)
            down(PAIRS, 0)

        @block.scalar
        def _(act):
            def copy(o, i_, signal):
                act.activation(o, i_, ACT.Copy).then_inc(signal, 1)

            def keep_xT(i, c, k):
                t, s, n = at(i, c, 2)
                act.wait_ge(xT_ps[s], k * uses(s) + n + 1)
                act.wait_ge(y_ps[s], k * uses(s) + n)
                copy(xTs[:, s].rearrange("p c n -> p (c n)"), psT[s][:, :], xT_sb[s])
                copy(kept(t), psT[s][:, :], xT_kept[s])

            def take_y(i, c, k):
                t, s, n = at(i, c, 2)
                act.wait_ge(y_ps[s], k * uses(s) + n + 1)
                act.wait_ge(y_st[s], 16 * (k * uses(s) + n))
                copy(outs[:, s, :], psY[s][:, :], y_sb[s])

            def give_xT(i, c, l):
                t, s, n = at(i, c, 2)
                act.wait_ge(z_ps[s], l * uses(s) + n)
                copy(xTs[:, s].rearrange("p c n -> p (c n)"), kept(t), xT_back[s])

            def high(i, c, l):
                t, g, n = at(i, c, 4)
                before = (g + 2) % 4
                act.wait_ge(edge_in[g], 16 * (l * uses(g) + n + 1))
                act.wait_ge(seg_ps[before], l * uses(before) + n + (g >= 2))
                copy(parts[:, g % 2, 0, :], rows[:, g, :], hi_set[g])

            def take_sums(i, c, l):
                t, g, n = at(i, c, 4)
                act.wait_ge(seg_ps[g], l * uses(g) + n + 1)
                act.wait_ge(seg_st[g], 16 * (l * uses(g) + n))
                copy(outs[:, g, :], psS[g % 2][:, :], seg_sb[g])

            for l in range(LAYERS):
                if l > 0:
                    for g in range(4):
                        act.wait_ge(seg_st[g], 16 * l * uses(g))
                    all_turns(act, z_ps, l)
                keep_xT(0, 0, l)
                for i in turns(act, PAIRS, l == 0):
                    for c in range(2):
                        keep_xT(i, c + 1, l)
                        take_y(i, c, l)
                take_y(PAIRS, 0, l)
                all_turns(act, xT_kept, l + 1)
                all_turns(act, y_st, l + 1, 16)
                give_xT(0, 0, l)
                high(0, 0, l)
                high(0, 1, l)
                for i in turns(act, PAIRS - 1, l == 0):
                    for c in range(2):
                        give_xT(i, c + 1, l)
                        for e in (2 * c, 2 * c + 1):
                            take_sums(i, e, l)
                            high(i, e + 2, l)
                give_xT(PAIRS - 1, 1, l)
                take_sums(PAIRS - 1, 0, l)
                high(PAIRS - 1, 2, l)
                take_sums(PAIRS - 1, 1, l)
                high(PAIRS - 1, 3, l)
                give_xT(PAIRS, 0, l)
                take_sums(PAIRS - 1, 2, l)
                high(PAIRS, 0, l)
                take_sums(PAIRS - 1, 3, l)
                take_sums(PAIRS, 0, l)

            def take_xT(i, c):
                t, s, n = at(i, c, 2)
                act.wait_ge(xT_ps[s], LAYERS * uses(s) + n + 1)
                act.wait_ge(y_ps[s], LAYERS * uses(s) + n)
                copy(xTs[:, s].rearrange("p c n -> p (c n)"), psT[s][:, :], xT_sb[s])

            def exps(i, c):
                t, s, n = at(i, c, 2)
                act.wait_ge(lg_sb[s], n + 1)
                act.activation(sm[:, s, EX:EX + X], sm[:, s, LG:LG + X], ACT.Exp, scale=-1.0,
                               bias=st[:, s, LOWEST:LOWEST + 1], accum_out=st[:, s, SUM:SUM + 1])\
                   .then_inc(p_sb[s], 1)

            def norm(i, c):
                t, s, n = at(i, c, 2)
                act.wait_ge(shift_in[s], n + 1)
                act.activation(rows[:, 2 + s, :], kept(t), ACT.Identity, scale=st[:, s, RSTD:RSTD + 1],
                               bias=st[:, s, SHIFT:SHIFT + 1]).then_inc(xn_ready[s], 1)

            def take_hT(i, c):
                t, s, n = at(i, c, 2)
                act.wait_ge(o_ps[s], n)
                act.wait_ge(hT_ps[s], n + 1)
                copy(hTs[:, s].rearrange("p c n -> p (c n)"), psS[0][:, :], hT_sb[s])
                act.wait_ge(cw_ps[s], n + 1)
                copy(cwT[:, s, :], psS[1][0:4 * X, 0:P], cw_sb[s])

            all_turns(act, z_ps, LAYERS)
            act.wait_ge(mend_ps, 2 * LAYERS)
            norm(0, 0)
            norm(0, 1)
            take_xT(0, 0)
            take_xT(0, 1)
            exps(0, 0)
            norm(0, 2)
            for i in turns(act, PAIRS - 1, True):
                for c in (1, 2):
                    take_xT(i, c + 1)
                    exps(i, c)
                    take_hT(i, c - 1)
                    norm(i, c + 2)
            take_xT(PAIRS - 1, 2)
            exps(PAIRS - 1, 1)
            take_hT(PAIRS - 1, 0)
            exps(PAIRS, 0)
            take_hT(PAIRS - 1, 1)
            take_hT(PAIRS, 0)

        @block.vector
        def _(dve):
            done = [0]

            def link(ins):
                done[0] += 1
                ins.then_inc(vchain, 1)
                dve.wait_ge(vchain, done[0])

            def linker(tile, per):
                k = [0]
                base = done[0]

                def one(ins):
                    k[0] += 1
                    ins.then_inc(vchain, 1)
                    dve.wait_ge(vchain, tile * per + (base + k[0]))
                    assert k[0] <= per
                return one

            def copy(o, i_):
                return dve.tensor_copy(o, i_)

            dve.wait_ge(ids_in, 96)
            dve.wait_ge(const_set, 10)
            for b, r in BLOCKS:
                dve.tensor_scalar(int_rows("lo", b)[0:r], int_rows("dst", b)[0:r], P - 1, None,
                                  ALU.bitwise_and).then_inc(vchain, 1)
                dve.tensor_scalar(int_rows("hi", b)[0:r], int_rows("dst", b)[0:r], 7, None,
                                  ALU.arith_shift_right).then_inc(vchain, 1)
                dve.tensor_copy(flt_rows("dst", b)[0:r], int_rows("dst", b)[0:r]).then_inc(vchain, 1)
                dve.tensor_copy(flt_rows("src", b)[0:r], int_rows("src", b)[0:r]).then_inc(vchain, 1)
            done[0] += 8
            dve.wait_ge(vchain, done[0])
            for b, r in BLOCKS:
                val, dstf = flt_rows("val", b), flt_rows("dst", b)
                dve.tensor_copy(flt_rows("lo", b)[0:r], int_rows("lo", b)[0:r]).then_inc(vchain, 1)
                dve.tensor_copy(flt_rows("hi", b)[0:r], int_rows("hi", b)[0:r]).then_inc(vchain, 1)
                dve.memset(val[0:r, 0:1], 0.0).then_inc(vchain, 1)
                dve.tensor_copy(op[0:r, b, DST:DST + 1], dstf[0:r, 0:1]).then_inc(vchain, 1)
                dve.tensor_tensor(val[0:r, 1:P], dstf[0:r, 1:P], dstf[0:r, 0:P - 1], ALU.not_equal)\
                   .then_inc(vchain, 1)
            done[0] += 10
            dve.wait_ge(vchain, done[0])
            for b, r in BLOCKS:
                val = flt_rows("val", b)
                dve.tensor_copy(op[0:r, b, LO:LO + 1], flt_rows("lo", b)[0:r, 0:1]).then_inc(vchain, 1)
                dve.tensor_copy(op[0:r, b, HI:HI + 1], flt_rows("hi", b)[0:r, 0:1]).then_inc(vchain, 1)
                dve.tensor_tensor(val[0:r, 1:P], val[0:r, 1:P], iota[0:r, 1:P], ALU.mult).then_inc(vchain, 1)
            done[0] += 6
            dve.wait_ge(vchain, done[0])
            for b, r in BLOCKS:
                val = flt_rows("val", b)
                link(dve.tensor_tensor_scan(flt_rows("head", b)[0:r], val[0:r], val[0:r], 0.0,
                                            ALU.max, ALU.max))
            dve.sem_inc(rows_set, 1)
            dve.wait_ge(lists_ps, 2)
            for b, r in BLOCKS:
                for k, table in enumerate((srcT[:, :], loT, hiT, headT[:, :])):
                    dve.tensor_copy(table[:, b * P:b * P + r], psS[b][:, k * P:k * P + r]).then_inc(vchain, 1)
            done[0] += 8
            dve.wait_ge(vchain, done[0])
            dve.sem_inc(lists_set, 1)

            dve.wait_ge(b2_in, 64)
            link(dve.tensor_scalar(group, group, 3, 1, ALU.arith_shift_right, ALU.bitwise_and))
            link(copy(is_low, group))
            link(dve.tensor_scalar(is_high, is_low, -1.0, 1.0, ALU.mult, ALU.add))
            link(copy(b2high.bitcast(F32R), b2raw))
            link(dve.tensor_tensor(b2raw, b2raw, b2high, ALU.subtract))
            link(dve.tensor_scalar(b2raw, b2raw, is_low, None, ALU.mult))
            dve.scalar_tensor_tensor(b2s[:, :], b2high, is_high, b2raw, ALU.mult, ALU.add).then_inc(b2_set, 1)

            def carry(k):
                dve.memset(scrap[:, k:k + 1], 0.0)

            def moments(s, node_rows, one):
                carry(0)
                one(dve.bn_stats(st[:, s, STAT:STAT + 6], node_rows))
                carry(1)
                one(dve.bn_aggr(st[:, s, MEAN:MEAN + 2], st[:, s, STAT:STAT + 6]))
                variance(s)

            def variance(s):
                var = st[:, s, VAR:VAR + 1]
                dve.tensor_scalar(var, var, EPS, None, ALU.add).then_inc(var_in[s], 1)

            def norm_x(i, c):
                t, s, n = at(i, c, 2)
                dve.wait_ge(x_in[s], 16 * (n + 1))
                moments(s, rows[:, s, :], linker(t, 2))

            def norm_x_end(i, c):
                t, s, n = at(i, c, 2)
                dve.wait_ge(xT_ps[s], n)
                dve.wait_ge(rstd_in[s], n + 1)
                dve.tensor_scalar(rows[:, 2 + s, :], rows[:, s, :], st[:, s, MEAN:MEAN + 1],
                                  st[:, s, RSTD:RSTD + 1], ALU.subtract, ALU.mult).then_inc(xn_ready[s], 1)

            def one_hot(i, c):
                t, g, n = at(i, c, 4)
                dve.wait_ge(oh_used[g], n)
                dve.tensor_scalar(onehot[:, g, 0:P], iota[:, :], col(loT, t), None, ALU.is_equal)\
                   .then_inc(oh_set[g], 1)
                dve.tensor_scalar(onehot[:, g, P:P + NT], iota[:, 0:NT], col(hiT, t), None, ALU.is_equal)\
                   .then_inc(oh_set[g], 1)

            norm_x(0, 0)
            for i in turns(dve, PAIRS, True):
                for c in range(2):
                    norm_x_end(i, c)
                    one_hot(i, 2 * c)
                    one_hot(i, 2 * c + 1)
                    norm_x(i, c + 1)
            norm_x_end(PAIRS, 0)
            one_hot(PAIRS, 0)
            done[0] += 2 * NT

            def make_plan():
                for g in range(4):
                    dve.wait_ge(oh_used[g], uses(g))
                link(copy(counts, psH[:, 0:NT]))
                link(dve.tensor_scalar(rdeg[:, :], counts, 1.0, None, ALU.max))
                link(dve.reciprocal(rdeg[:, :], rdeg[:, :]))
                link(dve.scalar_tensor_tensor(dstT, hiT, float(P), loT, ALU.mult, ALU.add))
                for b, r in BLOCKS:
                    link(dve.tensor_scalar(openlo[b][0:r, :], iota[0:r, :], op[0:r, b, LO:LO + 1], None,
                                           ALU.is_equal))
                dve.sem_inc(plan_in, 1)
                dve.wait_ge(plan_ps, 1)
                link(copy(colsum, psM[:, P:P + NT]))
                link(dve.tensor_tensor_scan(work, ones[:, 0:NT], colsum, 0.0, ALU.mult, ALU.add))
                link(dve.tensor_tensor(work, work, colsum, ALU.subtract))
                link(dve.tensor_tensor(starts, work, psM[:, 0:NT], ALU.add))
                for b, r in BLOCKS:
                    link(copy(openlo[b][:, 0:r], psH[:, (1 + b) * P:(1 + b) * P + r]))
                dve.sem_inc(plan_rp, 1)
                link(dve.tensor_scalar(work, counts, 0.0, None, ALU.is_gt))
                link(dve.scalar_tensor_tensor(work, starts, float(-ZERO), work, ALU.add, ALU.mult))
                link(dve.tensor_scalar(nodeI[:, :], work, float(ZERO), None, ALU.add))
                dve.wait_ge(plan_hf, 1)
                for b, r in BLOCKS:
                    def o(k):
                        return op[0:r, b, k:k + 1]
                    link(dve.scalar_tensor_tensor(work[0:r], iota[0:r, 0:NT], o(HI), psS[b][0:r, 0:NT],
                                                  ALU.is_equal, ALU.mult))
                    link(dve.tensor_reduce(o(HEAD), work[0:r], AX.X, ALU.add))
                    link(dve.tensor_tensor(o(BEGUN), o(HEAD), o(START), ALU.is_lt))
                    link(dve.tensor_scalar(o(PREV), o(START), float(-P), None, ALU.add))
                    link(dve.scalar_tensor_tensor(o(NEXT), o(HEAD), o(PREV), o(BEGUN), ALU.is_ge, ALU.mult))
                    link(copy(ixf[0:r, b:b + 1], o(HEAD)))
                    link(dve.scalar_tensor_tensor(o(NEXT), o(HEAD), float(-FAR), o(NEXT), ALU.add, ALU.mult))
                    link(dve.tensor_scalar(ixf[0:r, 2 + b:3 + b], o(NEXT), float(FAR), None, ALU.add))
                    link(dve.tensor_scalar(mendM[0:r, b, :], psM[0:r, 2 * P:2 * P + ET], o(DST), o(BEGUN),
                                           ALU.is_equal, ALU.mult))
                dve.sem_inc(plan_done, 1)

            def take_z(i, c, l):
                t, s, n = at(i, c, 2)
                dve.wait_ge(z_ps[s], l * uses(s) + n + 1)
                dve.tensor_tensor(kept(t), psY[s][:, :], bvec[:, :], ALU.add).then_inc(z_sb[s], 1)

            def select(i, c, l):
                t, g, n = at(i, c, 4)
                dve.wait_ge(seg_ps[g], l * uses(g) + n)
                dve.tensor_scalar(sel[:, g, :], iota[:, :], col(headT, t), None, ALU.is_equal)\
                   .then_inc(sel_set[g], 1)

            def low(i, c, l):
                t, g, n = at(i, c, 4)
                dve.wait_ge(hi_set[g], l * uses(g) + n + 1)
                dve.tensor_tensor(parts[:, g % 2, 1, :], rows[:, g, :], parts[:, g % 2, 0, :].bitcast(F32),
                                  ALU.subtract).then_inc(lo_set[g], 1)

            def next_x(i, c, k):
                t, s, n = at(i, c, 2)
                one = linker(t, 2)
                dve.wait_ge(node_in[s], 16 * ((k - 1) * uses(s) + n + 1))
                dve.wait_ge(xT_ps[s], k * uses(s) + n)
                a, v = rows[:, s, :], rows[:, 2 + s, :]
                one(dve.scalar_tensor_tensor(a, a, col(rdeg, t), kept(t), ALU.mult, ALU.add))
                one(dve.scalar_tensor_tensor(v, a, 0.0, avec[:, :], ALU.min, ALU.mult))
                dve.scalar_tensor_tensor(v, a, 0.0, v, ALU.max, ALU.add).then_inc(xn_ready[s], 1)

            for l in range(LAYERS):
                if l == 0:
                    make_plan()
                dve.wait_ge(bvec_in, 16 * (l + 1))
                for e in range(2):
                    select(0, e, l)
                    low(0, e, l)
                for i in turns(dve, PAIRS - 1, l == 0):
                    for c in range(2):
                        take_z(i, c, l)
                        for e in (2 * c + 2, 2 * c + 3):
                            select(i, e, l)
                            low(i, e, l)
                take_z(PAIRS - 1, 0, l)
                for e in (2, 3):
                    select(PAIRS - 1, e, l)
                    low(PAIRS - 1, e, l)
                take_z(PAIRS - 1, 1, l)
                select(PAIRS, 0, l)
                low(PAIRS, 0, l)
                take_z(PAIRS, 0, l)
                dve.wait_ge(mend_g, 32 * (l + 1))
                for b, r in BLOCKS:
                    dve.wait_ge(mend_ps, 2 * l + b + 1)
                    dve.tensor_tensor(rows[0:r, 2 + b, :], rows[0:r, 2 + b, :], psS[b][0:r, :], ALU.add)\
                       .then_inc(mend_add, 1)
                dve.wait_ge(avec_in, 16 * (l + 1))
                all_turns(dve, z_sb, l + 1)
                if l + 1 < LAYERS:
                    each_pair(dve, lambda i, c: next_x(i, c, l + 1), False)
                    done[0] += 2 * NT

            def experts(i, c, steps, ahead=True, own=True):
                step, after = steps
                t, s, n = at(i, c, 2)
                ta, _, na = at(i, c + 2, 2)
                a, v, q = rows[:, s, :], rows[:, 2 + s, :], outs[:, s, :]

                def stat(k, size=1):
                    return st[:, s, k:k + size]

                def gate(k, size=X):
                    return sm[:, s, k:k + size]

                if own:
                    dve.wait_ge(lg_ps[s], n + 1)
                    k_lg = step(dve.scalar_tensor_tensor(gate(LG), psM[:, 0:X], -1.0, bgs[:, :],
                                                         ALU.mult, ALU.subtract))
                if ahead:
                    dve.wait_ge(node_in[s], 16 * ((LAYERS - 1) * uses(s) + na + 1))
                    k_a = step(dve.scalar_tensor_tensor(a, a, col(rdeg, ta), kept(ta), ALU.mult, ALU.add))
                if own:
                    after(k_lg)
                    dve.tensor_reduce(stat(LOWEST), gate(LG), AX.X, ALU.min).then_inc(lg_sb[s], 1)
                if ahead:
                    after(k_a)
                    dve.wait_ge(xT_ps[s], LAYERS * uses(s) + na)
                    step(dve.scalar_tensor_tensor(v, a, 0.0, avec[:, :], ALU.min, ALU.mult))
                    dve.wait_ge(xe_in[s], 16 * (na + 1))
                    k_q = step(dve.scalar_tensor_tensor(q, a, 0.0, q, ALU.max, ALU.add))
                if own:
                    dve.wait_ge(p_sb[s], n + 1)
                    step(dve.reciprocal(stat(INV), stat(SUM)))
                    carry(0)
                    k_top = step(dve.max(gate(TOP), gate(EX)))
                if ahead:
                    after(k_q)
                    k_x = step(dve.tensor_tensor(kept(ta), q, v, ALU.add))
                if own:
                    after(k_top)
                    step(dve.tensor_scalar(stat(TOPW, 2), sm[:, s, TOP:TOP + 2], stat(INV), None, ALU.mult))
                    carry(1)
                    k_idx = step(dve.max_index(smi[:, :], gate(TOP), gate(EX)))
                if ahead:
                    after(k_x)
                    carry(2)
                    k_bn = step(dve.bn_stats(stat(STAT, 6), kept(ta)))
                if own:
                    after(k_idx)
                    k_cast = step(dve.tensor_copy(stat(IDX, 2), smi[:, 0:2]))
                if ahead:
                    after(k_bn)
                    carry(3)
                    k_var = step(dve.bn_aggr(stat(MEAN, 2), stat(STAT, 6)))
                if own:
                    after(k_cast)
                    step(dve.tensor_scalar(gate(LG), iota[:, 0:X], stat(IDX), stat(TOPW), ALU.is_equal, ALU.mult))
                    k_one = step(dve.tensor_scalar(gate(EX), iota[:, 0:X], stat(IDX + 1), stat(TOPW + 1),
                                                   ALU.is_equal, ALU.mult))
                if ahead:
                    after(k_var)
                    dve.tensor_scalar(stat(MEAN), stat(MEAN), -1.0, None, ALU.mult)
                    variance(s)
                if own:
                    after(k_one)
                    k_cw = step(dve.tensor_tensor(gate(CW), gate(LG), gate(EX), ALU.add))
                    h = outs[:, 2 + s, :]
                    h3 = h.rearrange("p (e f) -> p e f", e=X)
                    dve.wait_ge(y_ps[s], LAYERS * uses(s) + n + 1)
                    dve.wait_ge(hT_ps[s], n)
                    k_h = step(dve.tensor_tensor(h, psY[s][:, :], bvec[:, :], ALU.add))
                    high, low = (gate(k, 2 * X).rearrange("p (g e) -> p g e", g=2) for k in (HIGH, LOW))
                    twice = gate(CW).unsqueeze(1).to_broadcast([P, 2, X])
                    after(k_cw)
                    dve.wait_ge(cw_ps[s], n)
                    k_high = step(dve.tensor_copy(high.bitcast(F32R), twice))
                    after(k_h)
                    dve.scalar_tensor_tensor(h3, h3, 0.0, gate(CW).unsqueeze(2).to_broadcast([P, X, F]),
                                             ALU.max, ALU.mult).then_inc(hg_sb[s], 1)
                    after(k_high)
                    dve.tensor_tensor(low, twice, high, ALU.subtract).then_inc(cw_set[s], 1)

            def finish(i, c):
                t, s, n = at(i, c, 2)
                dve.wait_ge(o_ps[s], n + 1)
                dve.tensor_tensor(kept(t), psH[:, :], kept(t), ALU.add).then_inc(o_sb[s], 1)

            def numbered(turn, per, base):
                made = [0]

                def step(ins):
                    made[0] += 1
                    assert made[0] <= per
                    ins.then_inc(vchain, 1)
                    return made[0]

                def after(k):
                    dve.wait_ge(vchain, turn * per + (base + k))

                return step, after

            AHEAD, OWN = 6, 11
            dve.wait_ge(bvec_in, 16 * (LAYERS + 1))
            dve.wait_ge(small_in, 32)
            for t in range(2):
                experts(0, t - 2, numbered(t, AHEAD, done[0]), own=False)
            done[0] += 2 * AHEAD
            experts(0, 0, numbered(0, AHEAD + OWN, done[0]))
            done[0] += AHEAD + OWN
            for i in turns(dve, PAIRS - 1, True):
                for c in (1, 2):
                    experts(i, c, numbered(2 * i + (c - 1), AHEAD + OWN, done[0]))
                    finish(i, c - 1)
            done[0] += 2 * (PAIRS - 1) * (AHEAD + OWN)
            for c in (1, 2):
                experts(PAIRS - 1, c, numbered(c - 1, OWN, done[0]), ahead=False)
                finish(PAIRS - 1, c - 1)
            finish(PAIRS, 0)


_INS = ["x", "src", "dst"] + [f"L0_gnn_{k}{l}" for l in range(3) for k in ("Wl", "bl", "Wr", "a")] \
    + [f"L0_ffn_{k}" for k in ("Wr", "br", "W1", "b1", "W2", "b2")]


def kernel(**inputs):
    import numpy as _np
    import concourse.bacc as _bacc
    from concourse import mybir as _mybir
    from concourse.bass_utils import run_bass_kernel_spmd as _run

    nc = _bacc.Bacc("TRN2", target_bir_lowering=False, num_devices=1)
    arrays, aps = {}, {}
    for name in _INS:
        a = _np.ascontiguousarray(inputs[name])
        arrays[f"in_{name}"] = a
        aps[name] = nc.dram_tensor(f"in_{name}", a.shape, _mybir.dt.from_np(a.dtype), kind="ExternalInput").ap()
    out = nc.dram_tensor("out_rows", inputs["x"].shape, F32, kind="ExternalOutput").ap()
    gnn = {k: [aps[f"L0_gnn_{k}{l}"] for l in range(3)] for k in ("Wl", "bl", "Wr", "a")}
    build(nc, aps["x"], aps["src"], aps["dst"], gnn["Wl"], gnn["bl"], gnn["Wr"], gnn["a"],
          *(aps[f"L0_ffn_{k}"] for k in ("Wr", "br", "W1", "b1", "W2", "b2")), out)
    r = _run(nc, [arrays], core_ids=[0])
    return r.results[0]["out_rows"]
```

```python
from contextlib import ExitStack

import concourse.bass as bass
from concourse import mybir

ALU = mybir.AluOpType
ACT = mybir.ActivationFunctionType
AX = mybir.AxisListType
F32 = mybir.dt.float32
F32R = mybir.dt.float32r
BF16 = mybir.dt.bfloat16
I32 = mybir.dt.int32
U32 = mybir.dt.uint32

P = 128
EPS = 1e-5
FAR = 1 << 22


def at(i, c, ring):
    return i * ring + c, c % ring, i + c // ring


def build(nc, x, src, dst, Wl, bl, Wr, al, Wg, bg, W1, b1, W2, b2, out):
    N, D = x.shape
    E = src.shape[0]
    X = W1.shape[0]
    F = W1.shape[2]
    C = D // P
    LAYERS = len(Wl)
    NT = -(-N // P)
    ET = -(-E // P)
    ER = E - (ET - 1) * P
    NR = N - (NT - 1) * P
    PAIRS = NT // 2
    assert D == 512 and X * F == 512 and X == 8 and NT == 2 * PAIRS + 1 and ET == 4 * PAIRS + 1
    EB = ET - P
    ZERO = ET * P
    BLOCKS = [(0, P), (1, EB)]

    def uses(slot):
        return PAIRS + (slot == 0)

    y_d = nc.dram_tensor("y_rows", (NT * P, D), F32, kind="Internal").ap()
    s_d = nc.dram_tensor("sum_rows", (ET * P + 1, D), F32, kind="Internal").ap()

    with ExitStack() as ctx:
        def sb(name, shape, dt=F32):
            return ctx.enter_context(nc.sbuf_tensor(name, shape, dt))

        def pb(name, shape, dt=F32):
            return ctx.enter_context(nc.psum_tensor(name, shape, dt))

        def sem(name):
            return ctx.enter_context(nc.semaphore(name))

        def sems(name, n):
            return [sem(f"{name}{k}") for k in range(n)]

        res = sb("res", [P, NT, D])
        wy_at = nc.sbuf_base
        wy = sb("wy", [P, C, D])
        wz = sb("wz", [P, C, D])
        rows_at = nc.sbuf_base
        rows = sb("rows", [P, 4, D])
        outs = sb("outs", [P, 4, D])
        xTs = sb("xTs", [P, 2, C, P])
        hTs_at = nc.sbuf_base
        hTs = sb("hTs", [P, 2, C, P])
        bvec = sb("bvec", [P, D])
        avec = sb("avec", [P, D])
        b2s = sb("b2s", [4 * X, D], F32R)
        ident = sb("ident", [P, P])
        iota = sb("iota", [P, P])
        lists_at = nc.sbuf_base
        lists = sb("lists", [P, 2 * ET])
        nodeI = sb("nodeI", [P, NT], I32)
        rdeg = sb("rdeg", [P, NT])
        small = sb("small", [P, 15])
        ixe, ixn, ixf = (small[:, k:k + n].bitcast(I32) for k, n in ((0, 4), (4, 2), (6, 4)))
        half, scrap = small[:, 10:11], small[0:1, 11:15]
        wgs = sb("wgs", [P, C, X])
        bgs = sb("bgs", [P, X])
        st = sb("st", [P, 2, 17])
        sm = sb("sm", [P, 2, 8 * X])
        LG, EX, TOP, CW, HIGH, LOW = (X * k for k in (0, 1, 2, 3, 4, 6))
        STAT, MEAN, VAR, RSTD, SHIFT, LOWEST, SUM, INV, IDX, TOPW = 0, 6, 7, 8, 9, 10, 11, 12, 13, 15
        op = sb("op", [P, 2, 8])
        LO, HI, DST, START, HEAD, BEGUN, NEXT, PREV = range(8)

        hTs0 = hTs[:, 0].rearrange("p c n -> p (c n)")
        hTs1 = hTs[:, 1].rearrange("p c n -> p (c n)")
        srcT = lists[:, 0:ET].bitcast(I32)
        headT = lists[:, ET:2 * ET]
        cwT = nc.alloc_sbuf_tensor_at("cwT", [4 * X, 2, P], F32R, offset=lists_at)
        highs = nc.alloc_sbuf_tensor_at("highs", [P, 4, D], F32R, offset=wy_at)
        lows = nc.alloc_sbuf_tensor_at("lows", [P, 4, D], F32R, offset=rows_at)
        sel = nc.alloc_sbuf_tensor_at("sel", [P, 4, P], F32R, offset=hTs_at)
        lower, ones, first = (hTs[:, 0, k, :] for k in range(3))
        onehot = hTs1.bitcast(BF16).rearrange("p (g n) -> p g n", g=4)
        mendM = hTs1[:, 0:2 * ET].rearrange("p (b t) -> p b t", b=2)
        openlo = [hTs1[:, 320:320 + P], outs[:, 3, 320:320 + P]]
        loT = outs[:, 3, 0:ET]
        hiT = outs[:, 3, ET:2 * ET]
        counts, colsum, starts, work = (outs[:, 2, 80 * k:80 * k + NT] for k in range(4))
        dstT = outs[:, 2, 320:320 + ET]

        def tmp(k, n=P):
            return res[:, NT - 8 + k // 4, (k % 4) * P:(k % 4) * P + n]

        ints = {"src": (0, 1), "dst": (2, 3), "lo": (4, 5), "hi": (6, 7)}
        flts = {"src": (8, 9), "lo": (10, 11), "hi": (12, 13), "head": (14, 15), "dst": (16, 17), "val": (18, 19)}
        smi = lists[:, 2 * P:2 * P + 8].bitcast(U32)
        zeros = tmp(24, D)
        b2raw = tmp(20, D)[0:4 * X]
        b2high = tmp(28, D)[0:4 * X]
        group, is_low, is_high = (tmp(-4)[0:4 * X, k:k + 1] for k in range(3))
        group = group.bitcast(I32)

        def int_rows(name, b):
            return tmp(ints[name][b]).bitcast(I32)

        def flt_rows(name, b):
            return tmp(flts[name][b])

        psT = [pb(f"psT{s}", [P, D]) for s in range(2)]
        psY = [pb(f"psY{s}", [P, D]) for s in range(2)]
        psS = [pb(f"psS{s}", [P, D]) for s in range(2)]
        psH = pb("psH", [P, D])
        psM = pb("psM", [P, D])

        ids_pad = sem("ids_pad")
        ids_in = sem("ids_in")
        const_set = sem("const_set")
        small_in = sem("small_in")
        b2_in = sem("b2_in")
        b2_set = sem("b2_set")
        zero_set = sem("zero_set")
        zero_st = sem("zero_st")
        rows_set = sem("rows_set")
        lists_ps = sem("lists_ps")
        lists_set = sem("lists_set")
        plan_in = sem("plan_in")
        plan_ps = sem("plan_ps")
        plan_rp = sem("plan_rp")
        plan_hf = sem("plan_hf")
        plan_done = sem("plan_done")
        wy_in = sem("wy_in")
        wz_in = sem("wz_in")
        bvec_in = sem("bvec_in")
        avec_in = sem("avec_in")
        x_in = sems("x_in", 2)
        xe_in = sems("xe_in", 2)
        ix_n = sems("ix_n", 2)
        node_in = sems("node_in", 2)
        vchain = sem("vchain")
        xn_ready = sems("xn_ready", 2)
        xT_ps = sems("xT_ps", 2)
        xT_sb = sems("xT_sb", 2)
        xT_kept = sems("xT_kept", 2)
        y_ps = sems("y_ps", 2)
        y_sb = sems("y_sb", 2)
        y_st = sems("y_st", 2)
        var_in = sems("var_in", 2)
        rstd_in = sems("rstd_in", 2)
        shift_in = sems("shift_in", 2)
        oh_set = sems("oh_set", 4)
        oh_used = sems("oh_used", 4)
        ix_e = sems("ix_e", 4)
        edge_in = sems("edge_in", 4)
        hi_set = sems("hi_set", 4)
        lo_set = sems("lo_set", 4)
        sel_set = sems("sel_set", 4)
        seg_ps = sems("seg_ps", 4)
        seg_sb = sems("seg_sb", 4)
        seg_st = sems("seg_st", 4)
        xT_back = sems("xT_back", 2)
        z_ps = sems("z_ps", 2)
        z_sb = sems("z_sb", 2)
        mend_in = sems("mend_in", 2)
        mend_g = sems("mend_g", 2)
        mend_ps = sem("mend_ps")
        mend_add = sem("mend_add")
        mend_st = sem("mend_st")
        lg_ps = sems("lg_ps", 2)
        lg_sb = sems("lg_sb", 2)
        p_sb = sems("p_sb", 2)
        cw_set = sems("cw_set", 2)
        hg_sb = sems("hg_sb", 2)
        cw_ps = sems("cw_ps", 2)
        cw_sb = sems("cw_sb", 2)
        hT_ps = sems("hT_ps", 2)
        hT_sb = sems("hT_sb", 2)
        o_ps = sems("o_ps", 2)
        o_sb = sems("o_sb", 2)
        o_st = sems("o_st", 2)

        block = ctx.enter_context(nc.Block())

        def all_turns(eng, signals, rounds, step=1):
            for slot, s in enumerate(signals):
                eng.wait_ge(s, rounds * uses(slot) * step)

        def turns(eng, n, fresh):
            if fresh:
                yield 0
            with eng.Fori(1 if fresh else 0, n) as i:
                yield i

        def each_pair(eng, step, fresh):
            for i in turns(eng, PAIRS, fresh):
                for c in range(2):
                    step(i, c)
            step(PAIRS, 0)

        def each_four(eng, step, fresh):
            for i in turns(eng, PAIRS, fresh):
                for c in range(4):
                    step(i, c)
            step(PAIRS, 0)

        def edge_blocks(eng):
            yield (0, 1), [(0, 0), (0, 1)]
            yield (1, 0), [(0, 2), (0, 3)]
            yield (1, 1), [(1, 0), (1, 1)]
            with eng.Fori(2, PAIRS) as i:
                yield (i, 0), [(i, -2), (i, -1)]
                yield (i, 1), [(i, 0), (i, 1)]
            yield (PAIRS, 0), [(PAIRS - 1, 2), (PAIRS - 1, 3), (PAIRS, 0)]

        START_SLOT = (1, 0)
        MEND_SLOT = (2, 3)

        def stored(eng, b, l):
            for g in range(4):
                n = P // 4 if b == 0 else uses(g)
                eng.wait_ge(seg_st[g], 16 * (l * uses(g) + n))

        def two_on(edges):
            return [(i, c + 2) for i, c in edges if not (isinstance(i, int) and 4 * i + c + 2 >= ET)]

        def rows_of(t, n=P):
            return slice(t * P, t * P + n) if isinstance(t, int) else bass.ds(t * P, n)

        def kept(t, n=P):
            return res[0:n, t, :] if isinstance(t, int) else res[0:n, bass.ds(t, 1), :].rearrange("p a d -> p (a d)")

        def col(table, t):
            return table[:, t:t + 1] if isinstance(t, int) else table[:, bass.ds(t, 1)]

        def load_x(eng, i, c, ring, read, rounds, signal):
            t, s, n = at(i, c, 2)
            eng.wait_ge(read[s], rounds * uses(s) + n)
            r = NR if isinstance(t, int) and t == NT - 1 else P
            eng.dma_start(ring[0:r, s, :], x[rows_of(t, r)]).then_inc(signal[s], 16)

        @block.sync
        def _(sp):
            def load_w(buf, w, signal):
                sp.dma_start(buf[:, :, :], w.rearrange("(c p) n -> p c n", p=P)).then_inc(signal, 16)

            def load_row(buf, v, signal):
                sp.dma_start(buf[:, :], v.partition_broadcast(P)).then_inc(signal, 16)

            def store_y(i, c, k):
                t, s, n = at(i, c, 2)
                sp.wait_ge(y_sb[s], k * uses(s) + n + 1)
                sp.dma_start(y_d[rows_of(t)], outs[:, s, :]).then_inc(y_st[s], 16)

            sp.wait_ge(ids_pad, 2)
            for name, v in (("src", src), ("dst", dst)):
                sp.dma_start(int_rows(name, 0), v[0:P * P].rearrange("(t p) -> t p", p=P)).then_inc(ids_in, 16)
                sp.dma_start(int_rows(name, 1)[0:EB - 1], v[P * P:E - ER].rearrange("(t p) -> t p", p=P))\
                  .then_inc(ids_in, 16)
                sp.dma_start(int_rows(name, 1)[EB - 1:EB, 0:ER], v[E - ER:E].rearrange("(t p) -> t p", p=ER))\
                  .then_inc(ids_in, 16)
            load_w(wy, Wl[0], wy_in)
            for k in range(4):
                sp.dma_start(b2raw[k * X:(k + 1) * X, :], b2).then_inc(b2_in, 16)
            sp.wait_ge(zero_set, 1)
            sp.dma_start(s_d[ZERO:ZERO + 1], zeros[0:1, :]).then_inc(zero_st, 16)
            load_w(wz, Wr[0], wz_in)
            load_row(bvec, bl[0], bvec_in)
            load_row(avec, al[0], avec_in)
            load_row(bgs, bg, small_in)
            sp.dma_start(wgs[:, :, :], Wg.rearrange("(c p) n -> p c n", p=P)).then_inc(small_in, 16)
            each_pair(sp, lambda i, c: store_y(i, c, 0), True)

            def store_seg(i, c, l):
                t, g, n = at(i, c, 4)
                sp.wait_ge(seg_sb[g], l * uses(g) + n + 1)
                sp.dma_start(s_d[rows_of(t)], outs[:, g, :]).then_inc(seg_st[g], 16)

            for l in range(LAYERS):
                if l > 0:
                    all_turns(sp, xn_ready, l + 1)
                    load_row(avec, al[l], avec_in)
                each_four(sp, lambda i, c: store_seg(i, c, l), l == 0)
                starts_d = s_d[0:ET * P].rearrange("(t p) d -> t p d", p=P)[:, 0, :]
                for b, r in BLOCKS:
                    stored(sp, b, l)
                    if b == 0:
                        sp.wait_ge(seg_ps[START_SLOT[b]], (l + 1) * uses(START_SLOT[b]))
                    sp.dma_start(rows[0:r, START_SLOT[b], :], starts_d[b * P:b * P + r]).then_inc(mend_in[b], 16)
                if l + 1 < LAYERS:
                    load_w(wy, Wl[l + 1], wy_in)
                else:
                    for e in range(X):
                        sp.dma_start(wy[:, :, e * F:(e + 1) * F], W1[e].rearrange("(c p) f -> p c f", p=P))\
                          .then_inc(wy_in, 16)
                if l + 1 == LAYERS:
                    sp.wait_ge(mend_st, 32 * LAYERS)
                    for c in range(2):
                        load_x(sp, 0, c, outs, var_in, 1, xe_in)
                all_turns(sp, z_sb, l + 1)
                if l + 1 < LAYERS:
                    for i in turns(sp, PAIRS, True):
                        for c in range(2):
                            store_y(i, c, l + 1)
                        if isinstance(i, int):
                            load_w(wz, Wr[l + 1], wz_in)
                            load_row(bvec, bl[l + 1], bvec_in)
                    store_y(PAIRS, 0, l + 1)
                else:
                    load_row(bvec, b1.rearrange("e f -> (e f)"), bvec_in)
                    load_w(wz, W2.rearrange("e f d -> (e f) d"), wz_in)

            def store_out(i, c, r=P):
                t, s, n = at(i, c, 2)
                sp.wait_ge(o_sb[s], n + 1)
                sp.dma_start(out[rows_of(t, r)], kept(t, r)).then_inc(o_st[s], 16)

            for c in (2, 3):
                load_x(sp, 0, c, outs, var_in, 1, xe_in)
            for i in turns(sp, PAIRS - 2, True):
                for c in range(2):
                    load_x(sp, i, c + 4, outs, var_in, 1, xe_in)
                    store_out(i, c)
            load_x(sp, PAIRS, 0, outs, var_in, 1, xe_in)
            for c in range(4):
                store_out(PAIRS - 2, c)
            store_out(PAIRS, 0, NR)
            all_turns(sp, o_st, 1, 16)
            sp.wait_ge(zero_st, 16)

        @block.gpsimd
        def _(pool):
            pool.memset(int_rows("src", 1), 0).then_inc(ids_pad, 1)
            pool.memset(int_rows("dst", 1), -1).then_inc(ids_pad, 1)
            load_x(pool, 0, 0, rows, xn_ready, 0, x_in)
            load_x(pool, 0, 1, rows, xn_ready, 0, x_in)
            pool.iota(iota[:, :], pattern=[[1, P]], base=0, channel_multiplier=0,
                      allow_small_or_imprecise_dtypes=True).then_inc(const_set, 1)
            pool.memset(ident[:, :], 0.0).then_inc(const_set, 1)
            pool.memset(hTs0[:, 0:2 * P], 1.0).then_inc(const_set, 1)
            pool.memset(hTs0[:, 2 * P:3 * P], 0.0).then_inc(const_set, 1)
            pool.memset(zeros[0:1, :], 0.0).then_inc(zero_set, 1)
            pool.wait_ge(const_set, 4)
            pool.affine_select(out=ident[:, :], in_=ident[:, :], compare_op=ALU.not_equal, fill=1.0, base=0,
                               pattern=[[-1, P]], channel_multiplier=1).then_inc(const_set, 1)
            pool.affine_select(out=lower, in_=lower, compare_op=ALU.is_gt, fill=0.0, base=0,
                               pattern=[[1, P]], channel_multiplier=-1).then_inc(const_set, 1)
            pool.memset(first[0:1, :], 1.0).then_inc(const_set, 1)
            for b, r in BLOCKS:
                pool.iota(op[:, b, START:START + 1], pattern=[[0, 1]], base=b * P * P, channel_multiplier=P,
                          allow_small_or_imprecise_dtypes=True).then_inc(const_set, 1)

            pool.iota(group, pattern=[[0, 1]], base=0, channel_multiplier=1).then_inc(const_set, 1)
            pool.memset(half, -0.5).then_inc(const_set, 1)
            pool.wait_ge(const_set, 11)

            def rstd(i, c, k):
                t, s, n = at(i, c, 2)
                pool.wait_ge(var_in[s], k * uses(s) + n + 1)
                pool.tensor_tensor(st[:, s, RSTD:RSTD + 1], st[:, s, VAR:VAR + 1], half, ALU.pow)\
                    .then_inc(rstd_in[s], 1)

            for i in turns(pool, PAIRS - 1, True):
                for c in range(2):
                    rstd(i, c, 0)
                    load_x(pool, i, c + 2, rows, xn_ready, 0, x_in)
            rstd(PAIRS - 1, 0, 0)
            load_x(pool, PAIRS, 0, rows, xn_ready, 0, x_in)
            rstd(PAIRS - 1, 1, 0)
            rstd(PAIRS, 0, 0)

            def gather_edge(i, c, l):
                t, g, n = at(i, c, 4)
                used = l * uses(g) + n
                pool.wait_ge(seg_ps[g], used)
                pool.tensor_copy(ixe[:, g:g + 1], col(srcT, t)).then_inc(ix_e[g], 1)
                pool.wait_ge(ix_e[g], used + 1)
                pool.indirect_dma_start(out=rows[:, g, :], out_offset=None, in_=y_d,
                                        in_offset=bass.IndirectOffsetOnAxis(ap=ixe[:, g:g + 1], axis=0),
                                        bounds_check=i + (NT * P - 1 + c)).then_inc(edge_in[g], 16)

            def gather_node(i, c, l, read=xn_ready):
                t, s, n = at(i, c, 2)
                used = l * uses(s) + n
                pool.wait_ge(read[s], (uses(s) if read is var_in else (l + 1) * uses(s)) + n)
                pool.tensor_copy(ixn[:, s:s + 1], col(nodeI, t)).then_inc(ix_n[s], 1)
                pool.wait_ge(ix_n[s], used + 1)
                pool.indirect_dma_start(out=rows[:, s, :], out_offset=None, in_=s_d,
                                        in_offset=bass.IndirectOffsetOnAxis(ap=ixn[:, s:s + 1], axis=0),
                                        bounds_check=i + (ZERO + c)).then_inc(node_in[s], 16)

            for l in range(LAYERS):
                if l == 0:
                    pool.wait_ge(lists_set, 1)
                all_turns(pool, y_st, l + 1, 16)
                each_four(pool, lambda i, c: gather_edge(i, c, l), l == 0)
                if l == 0:
                    pool.wait_ge(plan_done, 1)
                    pool.wait_ge(zero_st, 16)
                for b, r in BLOCKS:
                    stored(pool, b, l)
                    g = MEND_SLOT[b]
                    pool.wait_ge(seg_ps[g], (l + 1) * uses(g))
                    last = P * P - 1 if b == 0 else ZERO
                    pool.indirect_dma_start(out=rows[0:r, g, :], out_offset=None, in_=s_d[0:last + 1],
                                            in_offset=bass.IndirectOffsetOnAxis(ap=ixf[0:r, b:b + 1], axis=0),
                                            bounds_check=last).then_inc(mend_g[b], 16)
                for b, r in BLOCKS:
                    pool.wait_ge(mend_in[b], 16 * (l + 1))
                    pool.wait_ge(mend_g[b], 16 * (l + 1))
                for b, r in BLOCKS:
                    pool.wait_ge(mend_add, 2 * l + b + 1)
                    pool.indirect_dma_start(out=s_d, out_offset=bass.IndirectOffsetOnAxis(
                                                ap=ixf[0:r, 2 + b:3 + b], axis=0),
                                            in_=rows[0:r, MEND_SLOT[b], :], in_offset=None,
                                            bounds_check=ZERO, oob_is_err=False).then_inc(mend_st, 16)
                pool.wait_ge(mend_st, 32 * (l + 1))
                if l + 1 < LAYERS:
                    each_pair(pool, lambda i, c: gather_node(i, c, l), l == 0)
            gather_node(0, 0, LAYERS - 1)
            gather_node(0, 1, LAYERS - 1)
            def scale_shift(i, c):
                t, s, n = at(i, c, 2)
                rstd(i, c, 1)
                pool.wait_ge(rstd_in[s], uses(s) + n + 1)
                pool.tensor_tensor(st[:, s, SHIFT:SHIFT + 1], st[:, s, MEAN:MEAN + 1], st[:, s, RSTD:RSTD + 1],
                                   ALU.mult).then_inc(shift_in[s], 1)

            for i in turns(pool, PAIRS - 1, True):
                for c in range(2):
                    scale_shift(i, c)
                    gather_node(i, c + 2, LAYERS - 1, var_in)
            scale_shift(PAIRS - 1, 0)
            gather_node(PAIRS, 0, LAYERS - 1, var_in)
            scale_shift(PAIRS - 1, 1)
            scale_shift(PAIRS, 0)

        @block.tensor
        def _(pe):
            def transposes(dest, tile, signal=None):
                for c in range(C):
                    mm = pe.transpose(dest[:, c * P:(c + 1) * P], tile[:, c * P:(c + 1) * P], ident[:, :])
                if signal is not None:
                    mm.then_inc(signal, 1)

            def product(dest, xT, w, signal=None, last=True):
                for c in range(C):
                    mm = pe.matmul(dest, xT[:, c, :], w[:, c, :], start=(c == 0), stop=(last and c == C - 1))
                if signal is not None:
                    mm.then_inc(signal, 1)

            def turn_lists():
                pe.wait_ge(rows_set, 1)
                for b, r in BLOCKS:
                    for k, name in enumerate(("src", "lo", "hi", "head")):
                        mm = pe.transpose(psS[b][:, k * P:k * P + r], flt_rows(name, b)[0:r, :], ident[0:r, 0:r])
                    mm.then_inc(lists_ps, 1)

            def x_transpose(i, c, k):
                t, s, n = at(i, c, 2)
                pe.wait_ge(xn_ready[s], k * uses(s) + n + 1)
                pe.wait_ge(xT_kept[s], k * uses(s) + n)
                transposes(psT[s], rows[:, 2 + s, :], xT_ps[s])

            def y_product(i, c, k):
                t, s, n = at(i, c, 2)
                pe.wait_ge(xT_sb[s], k * uses(s) + n + 1)
                pe.wait_ge(y_sb[s], k * uses(s) + n)
                product(psY[s][:, :], xTs[:, s], wy, y_ps[s])

            def count(i, c, start=False):
                t, g, n = at(i, c, 4)
                pe.wait_ge(oh_set[g], 2 * (n + 1))
                pe.matmul(psH[:, 0:NT], onehot[:, g, 0:P], onehot[:, g, P:P + NT], start=start, stop=True,
                          skip_group_check=True).then_inc(oh_used[g], 1)

            def dense(k):
                x_transpose(0, 0, k)
                if k == 0:
                    turn_lists()
                else:
                    all_turns(pe, z_sb, k)
                pe.wait_ge(wy_in, 16 * (k + 1))
                y_product(0, 0, k)
                if k == 0:
                    count(0, 0, True)
                    count(0, 1)
                    count(0, 2)
                x_transpose(0, 1, k)
                if k > 0:
                    x_transpose(0, 2, k)
                y_product(0, 1, k)
                if k == 0:
                    x_transpose(0, 2, k)
                    count(0, 3)
                    count(0, 4)
                with pe.Fori(1, PAIRS) as i:
                    for c in range(2):
                        x_transpose(i, c + 1, k)
                        y_product(i, c, k)
                        if k == 0:
                            count(i, 2 * c + 1)
                            count(i, 2 * c + 2)
                y_product(PAIRS, 0, k)

            def plan_counts():
                pe.wait_ge(plan_in, 1)
                pe.matmul(psM[:, 0:NT], lower, counts, start=True, stop=True)
                pe.matmul(psM[:, P:P + NT], ones, counts, start=True, stop=True)
                pe.matmul(psM[:, 2 * P:2 * P + ET], first, dstT, start=True, stop=True)
                for b, r in BLOCKS:
                    mm = pe.transpose(psH[:, (1 + b) * P:(1 + b) * P + r], openlo[b][0:r, :], ident[0:r, 0:r])
                mm.then_inc(plan_ps, 1)

            def plan_heads():
                pe.wait_ge(plan_rp, 1)
                for b, r in BLOCKS:
                    mm = pe.matmul(psS[b][0:r, 0:NT], openlo[b][:, 0:r], starts, start=True, stop=True)
                mm.then_inc(plan_hf, 1)

            def z_product(i, c, l):
                t, s, n = at(i, c, 2)
                pe.wait_ge(xT_back[s], l * uses(s) + n + 1)
                pe.wait_ge(z_sb[s], l * uses(s) + n)
                product(psY[s][:, :], xTs[:, s], wz, z_ps[s])

            def segment_sum(i, c, l):
                t, g, n = at(i, c, 4)
                used = l * uses(g) + n
                before = (g + 2) % 4
                pe.wait_ge(seg_sb[before], l * uses(before) + n + (g >= 2))
                pe.wait_ge(sel_set[g], used + 1)
                pe.wait_ge(hi_set[g], used + 1)
                pe.wait_ge(lo_set[g], used + 1)
                pe.matmul(psS[g % 2][:, :], sel[:, g, :], highs[:, g, :], start=True, stop=False)
                pe.matmul(psS[g % 2][:, :], sel[:, g, :], lows[:, g, :], start=False, stop=True)\
                  .then_inc(seg_ps[g], 1)

            pe.wait_ge(const_set, 10)
            for l in range(LAYERS):
                dense(l)
                if l == 0:
                    plan_counts()
                all_turns(pe, y_sb, l + 1)
                pe.wait_ge(wz_in, 16 * (l + 1))
                z_product(0, 0, l)
                if l == 0:
                    plan_heads()
                for node, edges in edge_blocks(pe):
                    z_product(*node, l)
                    for e in edges:
                        segment_sum(*e, l)
                for g in range(4):
                    pe.wait_ge(seg_sb[g], (l + 1) * uses(g))
                for b, r in BLOCKS:
                    for kb, kr in BLOCKS[b:]:
                        pe.wait_ge(mend_in[kb], 16 * (l + 1))
                        mm = pe.matmul(psS[b][0:r, :], mendM[0:kr, kb, b * P:b * P + r],
                                       rows[0:kr, START_SLOT[kb], :], start=(kb == b), stop=(kb == 1))
                    mm.then_inc(mend_ps, 1)

            def x_turn(i, c):
                t, s, n = at(i, c, 2)
                pe.wait_ge(xn_ready[s], LAYERS * uses(s) + n + 1)
                pe.wait_ge(xT_sb[s], LAYERS * uses(s) + n)
                transposes(psT[s], rows[:, 2 + s, :], xT_ps[s])

            def router(i, c, first=False):
                t, s, n = at(i, c, 2)
                pe.wait_ge(xT_sb[s], LAYERS * uses(s) + n + 1)
                _, so, no = at(i, c - 1, 2)
                if not first:
                    pe.wait_ge(lg_sb[so], no + 1)
                product(psM[:, 0:X], xTs[:, s], wgs, lg_ps[s])

            def up(i, c):
                t, s, n = at(i, c, 2)
                pe.wait_ge(hg_sb[s], n)
                product(psY[s][:, :], xTs[:, s], wy, y_ps[s])

            def hidden_turn(i, c, first=False):
                t, s, n = at(i, c, 2)
                _, so, no = at(i, c - 1, 2)
                pe.wait_ge(hg_sb[s], n + 1)
                if not first:
                    pe.wait_ge(hT_sb[so], no + 1)
                    pe.wait_ge(cw_sb[so], no + 1)
                transposes(psS[0], outs[:, 2 + s, :], hT_ps[s])
                pe.wait_ge(cw_set[s], n + 1)
                pe.transpose(psS[1][0:4 * X, 0:P], sm[:, s, HIGH:HIGH + 4 * X], ident[:, :])\
                  .then_inc(cw_ps[s], 1)

            def down(i, c, first=False):
                t, s, n = at(i, c, 2)
                _, so, no = at(i, c - 1, 2)
                if not first:
                    pe.wait_ge(o_sb[so], no + 1)
                pe.wait_ge(hT_sb[s], n + 1)
                product(psH[:, :], hTs[:, s], wz, last=False)
                pe.wait_ge(cw_sb[s], n + 1)
                pe.matmul(psH[:, :], cwT[:, s, :], b2s[:, :], start=False, stop=True).then_inc(o_ps[s], 1)

            pe.wait_ge(small_in, 32)
            x_turn(0, 0)
            all_turns(pe, z_sb, LAYERS)
            router(0, 0, True)
            pe.wait_ge(wy_in, 16 * (LAYERS + X))
            up(0, 0)
            x_turn(0, 1)
            pe.wait_ge(wz_in, 16 * (LAYERS + 1))
            pe.wait_ge(b2_set, 1)
            for i in turns(pe, PAIRS - 1, True):
                for c in (1, 2):
                    start = isinstance(i, int) and c == 1
                    x_turn(i, c + 1)
                    router(i, c)
                    hidden_turn(i, c - 1, start)
                    up(i, c)
                    down(i, c - 1, start)
            x_turn(PAIRS - 1, 2)
            for c in (1, 2):
                router(PAIRS - 1, c)
                hidden_turn(PAIRS - 1, c - 1)
                up(PAIRS - 1, c)
                down(PAIRS - 1, c - 1)
            hidden_turn(PAIRS, 0)
            down(PAIRS, 0)

        @block.scalar
        def _(act):
            def copy(o, i_, signal):
                act.activation(o, i_, ACT.Copy).then_inc(signal, 1)

            def keep_xT(i, c, k):
                t, s, n = at(i, c, 2)
                act.wait_ge(xT_ps[s], k * uses(s) + n + 1)
                act.wait_ge(y_ps[s], k * uses(s) + n)
                copy(xTs[:, s].rearrange("p c n -> p (c n)"), psT[s][:, :], xT_sb[s])
                copy(kept(t), psT[s][:, :], xT_kept[s])

            def take_y(i, c, k):
                t, s, n = at(i, c, 2)
                act.wait_ge(y_ps[s], k * uses(s) + n + 1)
                act.wait_ge(y_st[s], 16 * (k * uses(s) + n))
                copy(outs[:, s, :], psY[s][:, :], y_sb[s])

            def give_xT(i, c, l):
                t, s, n = at(i, c, 2)
                act.wait_ge(z_ps[s], l * uses(s) + n)
                copy(xTs[:, s].rearrange("p c n -> p (c n)"), kept(t), xT_back[s])

            def high(i, c, l):
                t, g, n = at(i, c, 4)
                act.wait_ge(edge_in[g], 16 * (l * uses(g) + n + 1))
                copy(highs[:, g, :], rows[:, g, :], hi_set[g])

            def take_sums(i, c, l):
                t, g, n = at(i, c, 4)
                act.wait_ge(seg_ps[g], l * uses(g) + n + 1)
                act.wait_ge(seg_st[g], 16 * (l * uses(g) + n))
                copy(outs[:, g, :], psS[g % 2][:, :], seg_sb[g])

            for l in range(LAYERS):
                if l > 0:
                    for g in range(4):
                        act.wait_ge(seg_st[g], 16 * l * uses(g))
                    all_turns(act, z_ps, l)
                keep_xT(0, 0, l)
                for i in turns(act, PAIRS, l == 0):
                    for c in range(2):
                        keep_xT(i, c + 1, l)
                        take_y(i, c, l)
                take_y(PAIRS, 0, l)
                all_turns(act, xT_kept, l + 1)
                give_xT(0, 0, l)
                give_xT(0, 1, l)
                all_turns(act, y_st, l + 1, 16)
                high(0, 0, l)
                high(0, 1, l)

                def block_of(node, edges):
                    i, c = node
                    if not (isinstance(i, int) and i == PAIRS):
                        give_xT(i, c + 1, l)
                    for e in two_on(edges)[:2]:
                        high(*e, l)
                    for e in edges:
                        take_sums(*e, l)
                    for e in two_on(edges)[2:]:
                        high(*e, l)

                for node, edges in edge_blocks(act):
                    block_of(node, edges)
            def take_xT(i, c):
                t, s, n = at(i, c, 2)
                act.wait_ge(xT_ps[s], LAYERS * uses(s) + n + 1)
                act.wait_ge(y_ps[s], LAYERS * uses(s) + n)
                copy(xTs[:, s].rearrange("p c n -> p (c n)"), psT[s][:, :], xT_sb[s])

            def exps(i, c):
                t, s, n = at(i, c, 2)
                act.wait_ge(lg_sb[s], n + 1)
                act.activation(sm[:, s, EX:EX + X], sm[:, s, LG:LG + X], ACT.Exp, scale=-1.0,
                               bias=st[:, s, LOWEST:LOWEST + 1], accum_out=st[:, s, SUM:SUM + 1])\
                   .then_inc(p_sb[s], 1)

            def norm(i, c):
                t, s, n = at(i, c, 2)
                act.wait_ge(shift_in[s], n + 1)
                act.activation(rows[:, 2 + s, :], kept(t), ACT.Identity, scale=st[:, s, RSTD:RSTD + 1],
                               bias=st[:, s, SHIFT:SHIFT + 1]).then_inc(xn_ready[s], 1)

            def take_hT(i, c):
                t, s, n = at(i, c, 2)
                act.wait_ge(o_ps[s], n)
                act.wait_ge(hT_ps[s], n + 1)
                copy(hTs[:, s].rearrange("p c n -> p (c n)"), psS[0][:, :], hT_sb[s])
                act.wait_ge(cw_ps[s], n + 1)
                copy(cwT[:, s, :], psS[1][0:4 * X, 0:P], cw_sb[s])

            all_turns(act, z_ps, LAYERS)
            act.wait_ge(mend_ps, 2 * LAYERS)
            norm(0, 0)
            take_xT(0, 0)
            norm(0, 1)
            exps(0, 0)
            take_xT(0, 1)
            norm(0, 2)
            for i in turns(act, PAIRS - 1, True):
                for c in (1, 2):
                    take_xT(i, c + 1)
                    exps(i, c)
                    take_hT(i, c - 1)
                    norm(i, c + 2)
            take_xT(PAIRS - 1, 2)
            exps(PAIRS - 1, 1)
            take_hT(PAIRS - 1, 0)
            exps(PAIRS, 0)
            take_hT(PAIRS - 1, 1)
            take_hT(PAIRS, 0)

        @block.vector
        def _(dve):
            done = [0]

            def link(ins):
                done[0] += 1
                ins.then_inc(vchain, 1)
                dve.wait_ge(vchain, done[0])

            def linker(tile, per):
                k = [0]
                base = done[0]

                def one(ins):
                    k[0] += 1
                    ins.then_inc(vchain, 1)
                    dve.wait_ge(vchain, tile * per + (base + k[0]))
                    assert k[0] <= per
                return one

            def copy(o, i_):
                return dve.tensor_copy(o, i_)

            def split_dst():
                dve.wait_ge(ids_in, 96)
                for b, r in BLOCKS:
                    dve.tensor_scalar(int_rows("lo", b)[0:r], int_rows("dst", b)[0:r], P - 1, None,
                                      ALU.bitwise_and).then_inc(vchain, 1)
                    dve.tensor_scalar(int_rows("hi", b)[0:r], int_rows("dst", b)[0:r], 7, None,
                                      ALU.arith_shift_right).then_inc(vchain, 1)
                    dve.tensor_copy(flt_rows("dst", b)[0:r], int_rows("dst", b)[0:r]).then_inc(vchain, 1)
                    dve.tensor_copy(flt_rows("src", b)[0:r], int_rows("src", b)[0:r]).then_inc(vchain, 1)
                done[0] += 8
                dve.wait_ge(vchain, done[0])

            def set_heads():
                dve.wait_ge(const_set, 10)
                for b, r in BLOCKS:
                    val, dstf = flt_rows("val", b), flt_rows("dst", b)
                    dve.tensor_copy(flt_rows("lo", b)[0:r], int_rows("lo", b)[0:r]).then_inc(vchain, 1)
                    dve.tensor_copy(flt_rows("hi", b)[0:r], int_rows("hi", b)[0:r]).then_inc(vchain, 1)
                    dve.memset(val[0:r, 0:1], 0.0).then_inc(vchain, 1)
                    dve.tensor_copy(op[0:r, b, DST:DST + 1], dstf[0:r, 0:1]).then_inc(vchain, 1)
                    dve.tensor_tensor(val[0:r, 1:P], dstf[0:r, 1:P], dstf[0:r, 0:P - 1], ALU.not_equal)\
                       .then_inc(vchain, 1)
                done[0] += 10
                dve.wait_ge(vchain, done[0])
                for b, r in BLOCKS:
                    val = flt_rows("val", b)
                    dve.tensor_copy(op[0:r, b, LO:LO + 1], flt_rows("lo", b)[0:r, 0:1]).then_inc(vchain, 1)
                    dve.tensor_copy(op[0:r, b, HI:HI + 1], flt_rows("hi", b)[0:r, 0:1]).then_inc(vchain, 1)
                    dve.tensor_tensor(val[0:r, 1:P], val[0:r, 1:P], iota[0:r, 1:P], ALU.mult).then_inc(vchain, 1)
                done[0] += 6
                dve.wait_ge(vchain, done[0])
                for b, r in BLOCKS:
                    val = flt_rows("val", b)
                    link(dve.tensor_tensor_scan(flt_rows("head", b)[0:r], val[0:r], val[0:r], 0.0,
                                                ALU.max, ALU.max))
                dve.sem_inc(rows_set, 1)

            def take_lists():
                dve.wait_ge(lists_ps, 2)
                for b, r in BLOCKS:
                    for k, table in enumerate((srcT[:, :], loT, hiT, headT[:, :])):
                        dve.tensor_copy(table[:, b * P:b * P + r], psS[b][:, k * P:k * P + r]).then_inc(vchain, 1)
                done[0] += 8
                dve.wait_ge(vchain, done[0])
                dve.sem_inc(lists_set, 1)

            def split_b2():
                dve.wait_ge(b2_in, 64)
                link(dve.tensor_scalar(group, group, 3, 1, ALU.arith_shift_right, ALU.bitwise_and))
                link(copy(is_low, group))
                link(dve.tensor_scalar(is_high, is_low, -1.0, 1.0, ALU.mult, ALU.add))
                link(copy(b2high.bitcast(F32R), b2raw))
                link(dve.tensor_tensor(b2raw, b2raw, b2high, ALU.subtract))
                link(dve.tensor_scalar(b2raw, b2raw, is_low, None, ALU.mult))
                dve.scalar_tensor_tensor(b2s[:, :], b2high, is_high, b2raw, ALU.mult, ALU.add).then_inc(b2_set, 1)

            def carry(k):
                dve.memset(scrap[:, k:k + 1], 0.0)

            def moments(s, node_rows, one):
                carry(0)
                one(dve.bn_stats(st[:, s, STAT:STAT + 6], node_rows))
                carry(1)
                one(dve.bn_aggr(st[:, s, MEAN:MEAN + 2], st[:, s, STAT:STAT + 6]))
                variance(s)

            def variance(s):
                var = st[:, s, VAR:VAR + 1]
                dve.tensor_scalar(var, var, EPS, None, ALU.add).then_inc(var_in[s], 1)

            def norm_x(i, c, one=None):
                t, s, n = at(i, c, 2)
                dve.wait_ge(x_in[s], 16 * (n + 1))
                moments(s, rows[:, s, :], one or linker(t, 2))

            def norm_x_end(i, c):
                t, s, n = at(i, c, 2)
                dve.wait_ge(xT_ps[s], n)
                dve.wait_ge(rstd_in[s], n + 1)
                dve.tensor_scalar(rows[:, 2 + s, :], rows[:, s, :], st[:, s, MEAN:MEAN + 1],
                                  st[:, s, RSTD:RSTD + 1], ALU.subtract, ALU.mult).then_inc(xn_ready[s], 1)

            def one_hot(i, c):
                t, g, n = at(i, c, 4)
                dve.wait_ge(oh_used[g], n)
                dve.tensor_scalar(onehot[:, g, 0:P], iota[:, :], col(loT, t), None, ALU.is_equal)\
                   .then_inc(oh_set[g], 1)
                dve.tensor_scalar(onehot[:, g, P:P + NT], iota[:, 0:NT], col(hiT, t), None, ALU.is_equal)\
                   .then_inc(oh_set[g], 1)

            norm_x(0, 0, link)
            split_dst()
            norm_x_end(0, 0)
            set_heads()
            norm_x(0, 1, link)
            norm_x_end(0, 1)
            take_lists()
            for c in range(4):
                one_hot(0, c)
            norm_x(0, 2, link)
            split_b2()
            done[0] -= 2 * 3
            with dve.Fori(1, PAIRS) as i:
                for c in range(2):
                    norm_x_end(i, c)
                    one_hot(i, 2 * c)
                    one_hot(i, 2 * c + 1)
                    norm_x(i, c + 1)
            norm_x_end(PAIRS, 0)
            one_hot(PAIRS, 0)
            done[0] += 2 * NT

            def make_plan():
                for g in range(4):
                    dve.wait_ge(oh_used[g], uses(g))
                link(copy(counts, psH[:, 0:NT]))
                link(dve.tensor_scalar(rdeg[:, :], counts, 1.0, None, ALU.max))
                link(dve.reciprocal(rdeg[:, :], rdeg[:, :]))
                link(dve.scalar_tensor_tensor(dstT, hiT, float(P), loT, ALU.mult, ALU.add))
                for b, r in BLOCKS:
                    link(dve.tensor_scalar(openlo[b][0:r, :], iota[0:r, :], op[0:r, b, LO:LO + 1], None,
                                           ALU.is_equal))
                dve.sem_inc(plan_in, 1)
                dve.wait_ge(plan_ps, 1)
                link(copy(colsum, psM[:, P:P + NT]))
                link(dve.tensor_tensor_scan(work, ones[:, 0:NT], colsum, 0.0, ALU.mult, ALU.add))
                link(dve.tensor_tensor(work, work, colsum, ALU.subtract))
                link(dve.tensor_tensor(starts, work, psM[:, 0:NT], ALU.add))
                for b, r in BLOCKS:
                    link(copy(openlo[b][:, 0:r], psH[:, (1 + b) * P:(1 + b) * P + r]))
                dve.sem_inc(plan_rp, 1)
                link(dve.tensor_scalar(work, counts, 0.0, None, ALU.is_gt))
                link(dve.scalar_tensor_tensor(work, starts, float(-ZERO), work, ALU.add, ALU.mult))
                link(dve.tensor_scalar(nodeI[:, :], work, float(ZERO), None, ALU.add))
                dve.wait_ge(plan_hf, 1)
                for b, r in BLOCKS:
                    def o(k):
                        return op[0:r, b, k:k + 1]
                    link(dve.scalar_tensor_tensor(work[0:r], iota[0:r, 0:NT], o(HI), psS[b][0:r, 0:NT],
                                                  ALU.is_equal, ALU.mult))
                    link(dve.tensor_reduce(o(HEAD), work[0:r], AX.X, ALU.add))
                    link(dve.tensor_tensor(o(BEGUN), o(HEAD), o(START), ALU.is_lt))
                    link(dve.tensor_scalar(o(PREV), o(START), float(-P), None, ALU.add))
                    link(dve.scalar_tensor_tensor(o(NEXT), o(HEAD), o(PREV), o(BEGUN), ALU.is_ge, ALU.mult))
                    link(copy(ixf[0:r, b:b + 1], o(HEAD)))
                    link(dve.scalar_tensor_tensor(o(NEXT), o(HEAD), float(-FAR), o(NEXT), ALU.add, ALU.mult))
                    link(dve.tensor_scalar(ixf[0:r, 2 + b:3 + b], o(NEXT), float(FAR), None, ALU.add))
                    link(dve.tensor_scalar(mendM[0:r, b, :], psM[0:r, 2 * P:2 * P + ET], o(DST), o(BEGUN),
                                           ALU.is_equal, ALU.mult))
                dve.sem_inc(plan_done, 1)

            def take_z(i, c, l):
                t, s, n = at(i, c, 2)
                dve.wait_ge(z_ps[s], l * uses(s) + n + 1)
                dve.tensor_tensor(kept(t), psY[s][:, :], bvec[:, :], ALU.add).then_inc(z_sb[s], 1)

            def select(i, c, l):
                t, g, n = at(i, c, 4)
                dve.wait_ge(seg_ps[g], l * uses(g) + n)
                dve.tensor_scalar(sel[:, g, :], iota[:, :], col(headT, t), None, ALU.is_equal)\
                   .then_inc(sel_set[g], 1)

            def low(i, c, l):
                t, g, n = at(i, c, 4)
                dve.wait_ge(hi_set[g], l * uses(g) + n + 1)
                dve.tensor_tensor(lows[:, g, :], rows[:, g, :], highs[:, g, :].bitcast(F32), ALU.subtract)\
                   .then_inc(lo_set[g], 1)

            def next_x(i, c, k):
                t, s, n = at(i, c, 2)
                one = linker(t, 2)
                dve.wait_ge(node_in[s], 16 * ((k - 1) * uses(s) + n + 1))
                dve.wait_ge(xT_ps[s], k * uses(s) + n)
                a, v = rows[:, s, :], rows[:, 2 + s, :]
                one(dve.scalar_tensor_tensor(a, a, col(rdeg, t), kept(t), ALU.mult, ALU.add))
                one(dve.scalar_tensor_tensor(v, a, 0.0, avec[:, :], ALU.min, ALU.mult))
                dve.scalar_tensor_tensor(v, a, 0.0, v, ALU.max, ALU.add).then_inc(xn_ready[s], 1)

            for l in range(LAYERS):
                if l == 0:
                    make_plan()
                dve.wait_ge(bvec_in, 16 * (l + 1))
                def part(e):
                    select(*e, l)
                    low(*e, l)

                def block_of(node, edges):
                    for e in two_on(edges)[:2]:
                        part(e)
                    take_z(*node, l)
                    for e in two_on(edges)[2:]:
                        part(e)

                take_z(0, 0, l)
                part((0, 0))
                part((0, 1))
                for node, edges in edge_blocks(dve):
                    block_of(node, edges)
                for b, r in BLOCKS:
                    g = MEND_SLOT[b]
                    dve.wait_ge(mend_g[b], 16 * (l + 1))
                    dve.wait_ge(mend_ps, 2 * l + b + 1)
                    dve.tensor_tensor(rows[0:r, g, :], rows[0:r, g, :], psS[b][0:r, :], ALU.add)\
                       .then_inc(mend_add, 1)
                dve.wait_ge(avec_in, 16 * (l + 1))
                all_turns(dve, z_sb, l + 1)
                if l + 1 < LAYERS:
                    each_pair(dve, lambda i, c: next_x(i, c, l + 1), False)
                    done[0] += 2 * NT

            def experts(i, c, steps, ahead=True, own=True):
                step, after = steps
                t, s, n = at(i, c, 2)
                ta, _, na = at(i, c + 2, 2)
                a, v, q = rows[:, s, :], rows[:, 2 + s, :], outs[:, s, :]

                def stat(k, size=1):
                    return st[:, s, k:k + size]

                def gate(k, size=X):
                    return sm[:, s, k:k + size]

                if own:
                    dve.wait_ge(lg_ps[s], n + 1)
                    k_lg = step(dve.scalar_tensor_tensor(gate(LG), psM[:, 0:X], -1.0, bgs[:, :],
                                                         ALU.mult, ALU.subtract))
                if ahead:
                    dve.wait_ge(node_in[s], 16 * ((LAYERS - 1) * uses(s) + na + 1))
                    k_a = step(dve.scalar_tensor_tensor(a, a, col(rdeg, ta), kept(ta), ALU.mult, ALU.add))
                if own:
                    after(k_lg)
                    dve.tensor_reduce(stat(LOWEST), gate(LG), AX.X, ALU.min).then_inc(lg_sb[s], 1)
                if ahead:
                    after(k_a)
                    dve.wait_ge(xT_ps[s], LAYERS * uses(s) + na)
                    step(dve.scalar_tensor_tensor(v, a, 0.0, avec[:, :], ALU.min, ALU.mult))
                    dve.wait_ge(xe_in[s], 16 * (na + 1))
                    k_q = step(dve.scalar_tensor_tensor(q, a, 0.0, q, ALU.max, ALU.add))
                if own:
                    dve.wait_ge(p_sb[s], n + 1)
                    step(dve.reciprocal(stat(INV), stat(SUM)))
                    carry(0)
                    k_top = step(dve.max(gate(TOP), gate(EX)))
                if ahead:
                    after(k_q)
                    k_x = step(dve.tensor_tensor(kept(ta), q, v, ALU.add))
                if own:
                    after(k_top)
                    step(dve.tensor_scalar(stat(TOPW, 2), sm[:, s, TOP:TOP + 2], stat(INV), None, ALU.mult))
                    carry(1)
                    k_idx = step(dve.max_index(smi[:, :], gate(TOP), gate(EX)))
                if ahead:
                    after(k_x)
                    carry(2)
                    k_bn = step(dve.bn_stats(stat(STAT, 6), kept(ta)))
                if own:
                    after(k_idx)
                    k_cast = step(dve.tensor_copy(stat(IDX, 2), smi[:, 0:2]))
                if ahead:
                    after(k_bn)
                    carry(3)
                    k_var = step(dve.bn_aggr(stat(MEAN, 2), stat(STAT, 6)))
                if own:
                    after(k_cast)
                    step(dve.tensor_scalar(gate(LG), iota[:, 0:X], stat(IDX), stat(TOPW), ALU.is_equal, ALU.mult))
                    k_one = step(dve.tensor_scalar(gate(EX), iota[:, 0:X], stat(IDX + 1), stat(TOPW + 1),
                                                   ALU.is_equal, ALU.mult))
                if ahead:
                    after(k_var)
                    dve.tensor_scalar(stat(MEAN), stat(MEAN), -1.0, None, ALU.mult)
                    variance(s)
                if own:
                    after(k_one)
                    k_cw = step(dve.tensor_tensor(gate(CW), gate(LG), gate(EX), ALU.add))
                    h = outs[:, 2 + s, :]
                    h3 = h.rearrange("p (e f) -> p e f", e=X)
                    dve.wait_ge(y_ps[s], LAYERS * uses(s) + n + 1)
                    dve.wait_ge(hT_ps[s], n)
                    k_h = step(dve.tensor_tensor(h, psY[s][:, :], bvec[:, :], ALU.add))
                    high, low = (gate(k, 2 * X).rearrange("p (g e) -> p g e", g=2) for k in (HIGH, LOW))
                    twice = gate(CW).unsqueeze(1).to_broadcast([P, 2, X])
                    after(k_cw)
                    dve.wait_ge(cw_ps[s], n)
                    k_high = step(dve.tensor_copy(high.bitcast(F32R), twice))
                    after(k_h)
                    dve.scalar_tensor_tensor(h3, h3, 0.0, gate(CW).unsqueeze(2).to_broadcast([P, X, F]),
                                             ALU.max, ALU.mult).then_inc(hg_sb[s], 1)
                    after(k_high)
                    dve.tensor_tensor(low, twice, high, ALU.subtract).then_inc(cw_set[s], 1)

            def finish(i, c):
                t, s, n = at(i, c, 2)
                dve.wait_ge(o_ps[s], n + 1)
                dve.tensor_tensor(kept(t), psH[:, :], kept(t), ALU.add).then_inc(o_sb[s], 1)

            def numbered(turn, per, base):
                made = [0]

                def step(ins):
                    made[0] += 1
                    assert made[0] <= per
                    ins.then_inc(vchain, 1)
                    return made[0]

                def after(k):
                    dve.wait_ge(vchain, turn * per + (base + k))

                return step, after

            AHEAD, OWN = 6, 11
            for t in range(2):
                experts(0, t - 2, numbered(t, AHEAD, done[0]), own=False)
            done[0] += 2 * AHEAD
            dve.wait_ge(bvec_in, 16 * (LAYERS + 1))
            dve.wait_ge(small_in, 32)
            experts(0, 0, numbered(0, AHEAD + OWN, done[0]))
            done[0] += AHEAD + OWN
            for i in turns(dve, PAIRS - 1, True):
                for c in (1, 2):
                    experts(i, c, numbered(2 * i + (c - 1), AHEAD + OWN, done[0]))
                    finish(i, c - 1)
            done[0] += 2 * (PAIRS - 1) * (AHEAD + OWN)
            for c in (1, 2):
                experts(PAIRS - 1, c, numbered(c - 1, OWN, done[0]), ahead=False)
                finish(PAIRS - 1, c - 1)
            finish(PAIRS, 0)


_INS = ["x", "src", "dst"] + [f"L0_gnn_{k}{l}" for l in range(3) for k in ("Wl", "bl", "Wr", "a")] \
    + [f"L0_ffn_{k}" for k in ("Wr", "br", "W1", "b1", "W2", "b2")]


def kernel(**inputs):
    import numpy as _np
    import concourse.bacc as _bacc
    from concourse import mybir as _mybir
    from concourse.bass_utils import run_bass_kernel_spmd as _run

    nc = _bacc.Bacc("TRN2", target_bir_lowering=False, num_devices=1)
    arrays, aps = {}, {}
    for name in _INS:
        a = _np.ascontiguousarray(inputs[name])
        arrays[f"in_{name}"] = a
        aps[name] = nc.dram_tensor(f"in_{name}", a.shape, _mybir.dt.from_np(a.dtype), kind="ExternalInput").ap()
    out = nc.dram_tensor("out_rows", inputs["x"].shape, F32, kind="ExternalOutput").ap()
    gnn = {k: [aps[f"L0_gnn_{k}{l}"] for l in range(3)] for k in ("Wl", "bl", "Wr", "a")}
    build(nc, aps["x"], aps["src"], aps["dst"], gnn["Wl"], gnn["bl"], gnn["Wr"], gnn["a"],
          *(aps[f"L0_ffn_{k}"] for k in ("Wr", "br", "W1", "b1", "W2", "b2")), out)
    r = _run(nc, [arrays], core_ids=[0])
    return r.results[0]["out_rows"]
```
